# Optimizing a Trainium2 kernel written in Bass

```python
import numpy as np
import jax
import jax.numpy as jnp

def _softmax(x, axis=-1):
    return jax.nn.softmax(x, axis=axis)

def _gelu(x):
    return jax.nn.gelu(x, approximate=True)

def _silu(x):
    return jax.nn.silu(x)

def _sigmoid(x):
    return jax.nn.sigmoid(x)

def _layernorm(x, axis=-1, eps=1e-05):
    m = jnp.mean(x, axis=axis, keepdims=True)
    v = jnp.var(x, axis=axis, keepdims=True)
    return (x - m) / jnp.sqrt(v + eps)

def _scatter_add(tgt, idx, src, axis=0):
    return tgt.at[idx].add(src)

def _segment_sum(src, seg, n):
    return jax.ops.segment_sum(src, seg, n)
kernel_name = 'mk_seq_preln_d1_jaxref_r2_230921'

def setup_inputs(seed: int=0):
    np.random.seed(seed)
    _w = jnp.asarray

    def _L0_attn_setup():
        import jax, jax.numpy as jnp
        from jax import lax
        import numpy as np
        B, S, D, H = (4, 1024, 512, 16)
        HD = D // H
        EPS = 1e-08
        LN_EPS = 1e-05
        key = jax.random.key(seed)
        ks = jax.random.split(key, 8)
        sc = 1.0 / np.sqrt(D)
        return {'x': jax.random.normal(ks[0], (B, S, D), jnp.float32), 'time_mix_r': jnp.full((1, 1, D), 0.5, jnp.float32), 'time_mix_k': jnp.full((1, 1, D), 0.5, jnp.float32), 'time_mix_v': jnp.full((1, 1, D), 0.5, jnp.float32), 'W_r': jax.random.normal(ks[1], (D, D), jnp.float32) * sc, 'W_k': jax.random.normal(ks[2], (D, D), jnp.float32) * sc, 'W_v': jax.random.normal(ks[3], (D, D), jnp.float32) * sc, 'W_o': jax.random.normal(ks[4], (D, D), jnp.float32) * sc, 'time_decay': jax.random.normal(ks[5], (H, HD), jnp.float32) * 0.1 - 5.0, 'time_first': jax.random.normal(ks[6], (H, HD), jnp.float32) * 0.1, 'ln_gamma': jnp.ones((D,), jnp.float32), 'ln_beta': jnp.zeros((D,), jnp.float32)}
    _L0_attn_in = _L0_attn_setup()

    def _L0_ffn_setup():
        import jax, jax.numpy as jnp
        import numpy as np
        D_MODEL = 512
        D_FF = 1408
        N_EXPERTS = 8
        key = jax.random.key(seed)
        k_in, k1, k2, k3 = jax.random.split(key, 4)
        scale = 0.02
        inputs = jax.random.normal(k_in, (4, N_EXPERTS * 1024, D_MODEL), dtype=jnp.float32)
        w1 = jax.random.normal(k1, (N_EXPERTS, D_MODEL, D_FF), dtype=jnp.float32) * scale
        w3 = jax.random.normal(k3, (N_EXPERTS, D_MODEL, D_FF), dtype=jnp.float32) * scale
        w2 = jax.random.normal(k2, (N_EXPERTS, D_FF, D_MODEL), dtype=jnp.float32) * scale
        return {'inputs': inputs, 'w1': w1, 'w3': w3, 'w2': w2}
    _L0_ffn_in = _L0_ffn_setup()
    _d = {'L0_attn_x': _L0_attn_in['x'], 'L0_attn_time_mix_r': _L0_attn_in['time_mix_r'], 'L0_attn_time_mix_k': _L0_attn_in['time_mix_k'], 'L0_attn_time_mix_v': _L0_attn_in['time_mix_v'], 'L0_attn_W_r': _L0_attn_in['W_r'], 'L0_attn_W_k': _L0_attn_in['W_k'], 'L0_attn_W_v': _L0_attn_in['W_v'], 'L0_attn_W_o': _L0_attn_in['W_o'], 'L0_attn_time_decay': _L0_attn_in['time_decay'], 'L0_attn_time_first': _L0_attn_in['time_first'], 'L0_attn_ln_gamma': _L0_attn_in['ln_gamma'], 'L0_attn_ln_beta': _L0_attn_in['ln_beta'], 'L0_ffn_w1': _L0_ffn_in['w1'], 'L0_ffn_w3': _L0_ffn_in['w3'], 'L0_ffn_w2': _L0_ffn_in['w2']}
    _x0 = _d['L0_attn_x']
    _d['L0_attn_x'] = jax.random.normal(jax.random.fold_in(jax.random.key(seed), 1), (4, 2048, 512), dtype=_x0.dtype)
    del _x0
    return _d

def reference(L0_attn_x, L0_attn_time_mix_r, L0_attn_time_mix_k, L0_attn_time_mix_v, L0_attn_W_r, L0_attn_W_k, L0_attn_W_v, L0_attn_W_o, L0_attn_time_decay, L0_attn_time_first, L0_attn_ln_gamma, L0_attn_ln_beta, L0_ffn_w1, L0_ffn_w3, L0_ffn_w2):

    def _L0_attn_ref(x, time_mix_r, time_mix_k, time_mix_v, W_r, W_k, W_v, W_o, time_decay, time_first, ln_gamma, ln_beta):
        import jax, jax.numpy as jnp
        from jax import lax
        import numpy as np
        B, S, D, H = (4, 1024, 512, 16)
        HD = D // H
        EPS = 1e-08
        LN_EPS = 1e-05
        b, s, d = x.shape
        h, hd = time_decay.shape
        shifted = jnp.pad(x[:, :-1, :], ((0, 0), (1, 0), (0, 0)))
        xr = x * time_mix_r + shifted * (1.0 - time_mix_r)
        xk = x * time_mix_k + shifted * (1.0 - time_mix_k)
        xv = x * time_mix_v + shifted * (1.0 - time_mix_v)
        r = (xr @ W_r.T).reshape(b, s, h, hd)
        k = (xk @ W_k.T).reshape(b, s, h, hd)
        v = (xv @ W_v.T).reshape(b, s, h, hd)
        w = -jnp.exp(time_decay)
        u = time_first

        def step(carry, kv):
            a, bst = carry
            kt, vt = kv
            wk = kt + u
            p = jnp.maximum(bst, wk)
            e1 = jnp.exp(bst - p)
            e2 = jnp.exp(wk - p)
            out = (e1 * a + e2 * vt) / (e1 + e2 + EPS)
            ww = bst + w
            p2 = jnp.maximum(ww, kt)
            e1b = jnp.exp(ww - p2)
            e2b = jnp.exp(kt - p2)
            a_new = e1b * a + e2b * vt
            b_new = p2 + jnp.log(e1b + e2b + EPS)
            return ((a_new, b_new), out)
        a0 = jnp.zeros((b, h, hd), x.dtype)
        b0 = jnp.full((b, h, hd), -1e+38, x.dtype)
        kT = jnp.moveaxis(k, 1, 0)
        vT = jnp.moveaxis(v, 1, 0)
        _, outs = lax.scan(step, (a0, b0), (kT, vT))
        wkv = jnp.moveaxis(outs, 0, 1)
        rwkv = jax.nn.sigmoid(r) * wkv
        mean = jnp.mean(rwkv, axis=(1, 3), keepdims=True)
        var = jnp.var(rwkv, axis=(1, 3), keepdims=True)
        normed = (rwkv - mean) * lax.rsqrt(var + LN_EPS)
        normed = normed * ln_gamma.reshape(1, 1, h, hd) + ln_beta.reshape(1, 1, h, hd)
        return normed.reshape(b, s, d) @ W_o.T

    def _L0_ffn_ref(inputs, w1, w3, w2):
        import jax, jax.numpy as jnp
        import numpy as np
        D_MODEL = 512
        D_FF = 1408
        N_EXPERTS = 8
        B, T, D = inputs.shape
        E = w1.shape[0]
        C = T // E
        x = inputs.reshape(B, E, C, D)
        gate = jnp.einsum('becd,edf->becf', x, w1)
        up = jnp.einsum('becd,edf->becf', x, w3)
        h = jax.nn.silu(gate) * up
        out = jnp.einsum('becf,efd->becd', h, w2)
        return out.reshape(B, T, D)
    x = L0_attn_x
    x = x + _L0_attn_ref(_layernorm(x, axis=-1), L0_attn_time_mix_r, L0_attn_time_mix_k, L0_attn_time_mix_v, L0_attn_W_r, L0_attn_W_k, L0_attn_W_v, L0_attn_W_o, L0_attn_time_decay, L0_attn_time_first, L0_attn_ln_gamma, L0_attn_ln_beta)
    x = x + _L0_ffn_ref(_layernorm(x, axis=-1), L0_ffn_w1, L0_ffn_w3, L0_ffn_w2)
    return x

_drawn_inputs = setup_inputs


def setup_inputs(seed=0):
    import zlib

    import numpy as np

    out = dict(_drawn_inputs(seed))
    spreads = {'L0_attn_time_mix_r': (0.5, 0.2),
     'L0_attn_time_mix_k': (0.5, 0.2),
     'L0_attn_time_mix_v': (0.5, 0.2),
     'L0_attn_ln_gamma': (1.0, 0.2),
     'L0_attn_ln_beta': (0.0, 0.1)}
    factors = {'L0_attn_time_decay': 31.984, 'L0_attn_time_first': 54.661}
    for name, (base, spread) in spreads.items():
        noise = np.random.default_rng([zlib.crc32(name.encode()), seed]).standard_normal(out[name].shape)
        drawn = base * np.exp(spread * noise) if base else spread * noise
        out[name] = jnp.asarray(drawn.astype(out[name].dtype))
    for name, factor in factors.items():
        out[name] = (out[name] * factor).astype(out[name].dtype)
    return out
```

```python
from contextlib import ExitStack

import concourse.bass as bass
from concourse import mybir

ALU = mybir.AluOpType
ACT = mybir.ActivationFunctionType
F32 = mybir.dt.float32
F32R = mybir.dt.float32r

P = 128
T = 512
EPS = 1e-8
LN_EPS = 1e-5
LOWEST = -1e38
LOG_EXP = "natural_log_exp_and_others"
KIND_K, KIND_V, KIND_R = range(3)


def known(count):
    return max(count, 0) if isinstance(count, int) else count


FREE = 4


class Step:

    def __init__(self, b, i, per_batch):
        self.b, self.i, self.per_batch = b, i, per_batch

    def nth(self, n, of, ahead=0):
        return self.b * (self.per_batch * of) + ((self.i + ahead) * of + n)


def time_mixing(nc, sem, x, mix_in, wT_in, decay_in, first_in, gamma_in, beta_in, x2):
    B, S, D = x.shape
    C = D // P
    HD = 32
    NB = S // T
    TT = T // P
    
    with ExitStack() as ctx:
        def sb(name, shape, dt=F32):
            return ctx.enter_context(nc.sbuf_tensor(name, shape, dt))

        def psum(name, shape):
            return ctx.enter_context(nc.psum_tensor(name, shape, F32))

        w_hi = sb("w_hi", [P, 4, C, D], F32R)
        w_lo = sb("w_lo", [P, 4, C, D], F32R)
        ident = sb("ident", [P, P])
        same_head = sb("same_head", [P, P])
        eps = sb("eps", [P, 1])
        ln_eps = sb("ln_eps", [P, 1])
        mixc = sb("mixc", [P, 3, C])
        decay = sb("decay", [P, C])
        neg_decay = sb("neg_decay", [P, C])
        bonus = sb("bonus", [P, C])
        neg_bonus = sb("neg_bonus", [P, C])
        gamma = sb("gamma", [P, C])
        beta = sb("beta", [P, C])
        xin = sb("xin", [P, 2, D])
        bn_x = sb("bn_x", [P, 2, 6])
        mv_x = sb("mv_x", [P, 2, 2])
        ln_x = sb("ln_x", [P, 2])
        rstd_x = sb("rstd_x", [P, 2])
        xT = sb("xT", [P, C, 1 + T])
        xd = sb("xd", [P, C, T])
        mixed = sb("mixed", [P, 2, T])
        mix_hi = sb("mix_hi", [P, C, T], F32R)
        mix_lo = sb("mix_lo", [P, C, T], F32R)
        kk = sb("kk", [P, C, T])
        vv = sb("vv", [P, C, T])
        sig = sb("sig", [P, C, T])
        M = sb("M", [P, 2, 1 + T])
        A = sb("A", [P, 2, T])
        E = sb("E", [P, 2, T])
        S_ = sb("S_", [P, 2, 1 + T])
        acc = sb("acc", [P, 2, 1 + T])
        peak_c = sb("peak_c", [P, C])
        mass_c = sb("mass_c", [P, C])
        logm_c = sb("logm_c", [P, C])
        acc_c = sb("acc_c", [P, C])
        rw = sb("rw", [P, C, S])
        bn_rw = sb("bn_rw", [P, C, NB, 6])
        mv_rw = sb("mv_rw", [P, 2, C])
        mv_head = sb("mv_head", [P, 2, C])
        dev = sb("dev", [P, C])
        dev2 = sb("dev2", [P, C])
        var_h = sb("var_h", [P, C])
        ln_h = sb("ln_h", [P, C])
        rstd_h = sb("rstd_h", [P, C])
        scale_h = sb("scale_h", [P, C])
        mean_s = sb("mean_s", [P, C])
        shift_h = sb("shift_h", [P, C])
        y_hi = sb("y_hi", [P, 2, C, T // 2], F32R)
        y_lo = sb("y_lo", [P, 2, C, T // 2], F32R)
        xres = sb("xres", [P, 2, D])
        xout = sb("xout", [P, 2, D])

        acc_ps = [psum(f"acc_ps{g}", [P, T]) for g in range(C)]
        tp_ps = [psum(f"tp_ps{n}", [P, C, P]) for n in range(2)]
        out_ps = [psum(f"out_ps{n}", [P, D]) for n in range(2)]

        passed = sem("passed")
        const_loaded, w_loaded = sem("const_loaded"), sem("w_loaded")
        acc_start = sem("acc_start")
        x_loaded, xres_loaded, x2_stored = (
            [sem(f"{name}{n}") for n in range(2)] for name in ("x_loaded", "xres_loaded", "x2_stored"))
        (ident_zero, ident_made, w_hi_made, w_lo_made, decay_exp, const_made, bonus_neg) = map(
            sem, ("ident_zero", "ident_made", "w_hi_made", "w_lo_made", "decay_exp", "const_made", "bonus_neg"))
        (xbn, xstat, xlog, xrstd, xnormed, x_turned, shift_kept, xT_made, diff_made) = map(
            sem, ("xbn", "xstat", "xlog", "xrstd", "xnormed", "x_turned", "shift_kept", "xT_made", "diff_made"))
        (mix_made, hi_made, lo_made, chunk_used, kind_summed, kind_out) = map(
            sem, ("mix_made", "hi_made", "lo_made", "chunk_used", "kind_summed", "kind_out"))
        (start_set, peak_in, peak_made, peak_kept, fade_arg, fade_made, fresh_arg, fresh_made,
         mass_made, mass_kept, log_made, logm_in, logm_made, logm_kept, gap_made) = map(
            sem, ("start_set", "peak_in", "peak_made", "peak_kept", "fade_arg", "fade_made", "fresh_arg", "fresh_made",
                  "mass_made", "mass_kept", "log_made", "logm_in", "logm_made", "logm_kept", "gap_made"))
        (keep_made, add_made, e1_made, e2_made, keep_arg, addv_made, acc_in, acc_made, acc_kept,
         e1_arg, e2_arg, add_arg, den_made, e1a_made, e2v_made, num_made, gated, den_log, den_inv, rw_made, rw_bn) = map(
            sem, ("keep_made", "add_made", "e1_made", "e2_made", "keep_arg", "addv_made", "acc_in", "acc_made", "acc_kept",
                  "e1_arg", "e2_arg", "add_arg", "den_made", "e1a_made", "e2v_made", "num_made", "gated", "den_log", "den_inv",
                  "rw_made", "rw_bn"))
        (chan_stats, head_sum, head_copied, dev_made, dev_sq, dev_sum, head_var, head_log, head_rstd,
         scale_made, shift_mul, shift_made, y_made, yhi_made, ylo_made, out_summed, x2_made) = map(
            sem, ("chan_stats", "head_sum", "head_copied", "dev_made", "dev_sq", "dev_sum", "head_var", "head_log",
                  "head_rstd", "scale_made", "shift_mul", "shift_made", "y_made", "yhi_made", "ylo_made",
                  "out_summed", "x2_made"))

        x_tiles = x.rearrange("b (n p) d -> (b n) p d", p=P)
        x2_tiles = x2.rearrange("(n p) d -> n p d", p=P)
        stage = rw[:, :, 0:D]

        def whole(program, eng):
            program(0, True, True, False)
            with eng.Fori(1, B - 1) as b:
                program(b, True, True, True)
            program(B - 1, True, False, True)
            program(B, False, False, True)


        def groups(s, g):
            if g > 0:
                return s, g - 1
            if isinstance(s.b, int) and s.b == 0 and s.i == 0:
                return None, None
            return Step(s.b, s.i - 1, NB), C - 1

        block = ctx.enter_context(nc.Block())

        @block.sync
        def _(sp):
            with nc.allow_non_contiguous_dma(reason="per-channel vectors, once"):
                for n, m in enumerate(mix_in):
                    sp.dma_start(mixc[:, n, :], m.rearrange("(c p) -> p c", p=P)).then_inc(const_loaded, 16)
                for tile, src in ((decay, decay_in), (bonus, first_in), (gamma, gamma_in), (beta, beta_in)):
                    sp.dma_start(tile[:], src.rearrange("(c p) -> p c", p=P)).then_inc(const_loaded, 16)

            def load_x(s, n, ahead):
                sp.wait_ge(x_turned, known(s.nth(n - 1, TT, ahead)))
                tile = x_tiles[bass.ds(s.b * (NB * TT) + ((s.i + ahead) * TT + n), 1)]
                sp.dma_start(xin[:, n % 2:n % 2 + 1, :], tile.rearrange("o p d -> p o d")).then_inc(x_loaded[n % 2], 16)

            first = Step(0, 0, NB)
            load_x(first, 0, 0)
            load_x(first, 1, 0)
            for n in range(4):
                sp.wait_ge(w_lo_made, C * n)
                sp.dma_start(stage, wT_in[n].rearrange("(c p) d -> p c d", p=P)).then_inc(w_loaded, 16)
                if n == 0:
                    load_x(first, 2, 0)
                    load_x(first, 3, 0)
            load_x(first, 0, 1)
            load_x(first, 1, 1)
            for stored in x2_stored:
                sp.sem_inc(stored, 16 * FREE)

            def program(b, here, more, behind):
                for i in range(NB):
                    s = Step(b, i, NB)
                    if here and (more or i < NB - 1):
                        load_x(s, 2, 1)
                        load_x(s, 3, 1)
                    if here and (more or i < NB - 2):
                        load_x(s, 0, 2)
                        load_x(s, 1, 2)
                    if behind:
                        for n in range(TT + 2):
                            if n < TT:
                                sp.wait_ge(x2_made, known(s.nth(n - 1, TT, -NB) + FREE))
                                tile = x_tiles[bass.ds(b * (NB * TT) + ((i - NB) * TT + n), 1)]
                                sp.dma_start(xres[:, n % 2:n % 2 + 1, :],
                                             tile.rearrange("o p d -> p o d")).then_inc(xres_loaded[n % 2], 16)
                            if n >= 2:
                                sp.wait_ge(x2_made, known(s.nth(n - 1, TT, -NB) + FREE))
                                tile = x2_tiles[bass.ds(b * (NB * TT) + ((i - NB) * TT + n - 2), 1)]
                                sp.dma_start(tile.rearrange("o p d -> p o d"),
                                             xout[:, n % 2:n % 2 + 1, :]).then_inc(x2_stored[n % 2], 16)

            whole(program, sp)
            for stored in x2_stored:
                sp.wait_ge(stored, 16 * (B * NB * TT // 2 + FREE))

        @block.gpsimd
        def _(pool):
            g_ = nc.gpsimd
            g_.memset(ident[:], 0.0).then_inc(ident_zero, 1)
            g_.memset(same_head[:], 1.0 / HD).then_inc(ident_zero, 1)
            pool.wait_ge(ident_zero, 2)
            g_.affine_select(out=ident[:], in_=ident[:], compare_op=ALU.not_equal, fill=1.0, base=0,
                             pattern=[[-1, P]], channel_multiplier=1).then_inc(ident_made, 1)
            heads = same_head[:].rearrange("p (h k) -> p h k", k=HD)
            g_.affine_select(out=heads, in_=heads, compare_op=ALU.is_ge, fill=0.0, base=0,
                             pattern=[[-HD, P // HD], [0, HD]], channel_multiplier=1).then_inc(ident_made, 1)
            pool.wait_ge(ident_made, 2)
            g_.affine_select(out=heads, in_=heads, compare_op=ALU.is_ge, fill=0.0, base=HD - 1,
                             pattern=[[HD, P // HD], [0, HD]], channel_multiplier=-1).then_inc(ident_made, 1)
            for n in range(4):
                for c in range(C):
                    pool.wait_ge(w_hi_made, C * n + c + 1)
                    g_.tensor_tensor(w_lo[:, n, c, :], stage[:, c, :], w_hi[:, n, c, :].bitcast(F32),
                                     ALU.subtract).then_inc(w_lo_made, 1)

            def mix_low(s, kind, ahead, c):
                pool.wait_ge(hi_made, known(s.nth(C * kind + c + 1, 3 * C, ahead)))
                g_.tensor_tensor(mix_lo[:, c, :], mixed[:, c % 2, :], mix_hi[:, c, :].bitcast(F32),
                                 ALU.subtract).then_inc(lo_made, 1)

            def fresh_argument(s, g):
                pool.wait_ge(peak_made, known(s.nth(g + 1, C)))
                pool.wait_ge(acc_made, known(s.nth(g - 1, C)))
                g_.tensor_tensor(E[:, g % 2, :], kk[:, g, :], M[:, g % 2, 1:], ALU.subtract).then_inc(fresh_arg, 1)

            def log_mass(s, g):
                pool.wait_ge(log_made, known(s.nth(g + 1, C)))
                g_.tensor_tensor(S_[:, g % 2, 1:], M[:, g % 2, 1:], S_[:, g % 2, 1:], ALU.add).then_inc(logm_made, 1)

            def weigh(s, g):
                pool.wait_ge(den_made, known(s.nth(g + 1, C)))
                pool.wait_ge(acc_kept, known(s.nth(g + 1, C)))
                g_.tensor_tensor(S_[:, g % 2, 1:], S_[:, g % 2, 1:], acc[:, g % 2, 0:T], ALU.mult).then_inc(e1a_made, 1)
                g_.tensor_tensor(M[:, g % 2, 0:T], M[:, g % 2, 0:T], vv[:, g, :], ALU.mult).then_inc(e2v_made, 1)

            def gate(s, g):
                pool.wait_ge(kind_out, known(s.nth(C * KIND_R + g + 1, 3 * C)))
                pool.wait_ge(den_inv, known(s.nth(g + 1, C)))
                g_.tensor_tensor(A[:, g % 2, :], A[:, g % 2, :], sig[:, g, :], ALU.mult).then_inc(gated, 1)

            def y_low(s):
                for h in range(2):
                    pool.wait_ge(yhi_made, known(s.nth(h + 1, 2, -NB)))
                    g_.tensor_tensor(y_lo[:, h], rw[:, :, s.i * T + h * T // 2:s.i * T + (h + 1) * T // 2],
                                     y_hi[:, h].bitcast(F32), ALU.subtract).then_inc(ylo_made, 1)

            def program(b, here, more, behind):
                for i in range(NB):
                    s = Step(b, i, NB)
                    ahead = here and (more or i < NB - 1)
                    for g in range(C):
                        sb_, gb = groups(s, g)
                        back = sb_ is not None and (here or (i == 0 and g == 0))
                        kind, by = {0: (KIND_R, 0), 1: (None, 0), 2: (KIND_K, 1), 3: (KIND_V, 1)}[g]
                        mixing = kind is not None and (ahead if by else here)
                        if here:
                            fresh_argument(s, g)
                        if back:
                            weigh(sb_, gb)
                        if mixing:
                            mix_low(s, kind, by, 0)
                        if here:
                            log_mass(s, g)
                        if mixing:
                            mix_low(s, kind, by, 1)
                        if behind and g == 1 and i == 0:
                            y_low(s)
                        if back:
                            gate(sb_, gb)
                        if mixing:
                            mix_low(s, kind, by, 2)
                            mix_low(s, kind, by, 3)
                        if behind and g == 0 and i > 0:
                            y_low(s)

            first = Step(0, 0, NB)
            for kind in (KIND_K, KIND_V):
                for c in range(C):
                    mix_low(first, kind, 0, c)
            whole(program, pool)

        @block.tensor
        def _(pe):
            def turn(s, n, ahead=0):
                pe.wait_ge(xnormed, known(s.nth(n + 1, TT, ahead)))
                pe.wait_ge(xT_made, known(s.nth(n - 1, TT, ahead)))
                for c in range(C):
                    mm = pe.transpose(tp_ps[n % 2][:, c, :], xin[:, n % 2, c * P:(c + 1) * P], ident[:])
                mm.then_inc(x_turned, 1)

            def project(s, kind, ahead=0):
                for c in range(C):
                    pe.wait_ge(lo_made, known(s.nth(C * kind + c + 1, 3 * C, ahead)))
                    for g in range(C):
                        if c == 0:
                            pe.wait_ge(kind_out, known(s.nth(C * kind + g + 1 - C, 3 * C, ahead)))
                        cols = slice(g * P, (g + 1) * P)
                        hi, lo = w_hi[:, kind, c, cols], w_lo[:, kind, c, cols]
                        pe.matmul(acc_ps[g][:], hi, mix_hi[:, c, :], start=(c == 0), stop=False)
                        pe.matmul(acc_ps[g][:], hi, mix_lo[:, c, :], start=False, stop=False)
                        mm = pe.matmul(acc_ps[g][:], lo, mix_hi[:, c, :], start=False, stop=(c == C - 1))
                        if c == C - 1:
                            mm.then_inc(kind_summed, 1)
                    if c < C - 1:
                        mm.then_inc(chunk_used, 1)

            def head_sums(b):
                pe.wait_ge(chan_stats, b * 1)
                pe.wait_ge(x2_made, known(Step(b, 0, NB).nth(-1, TT, -NB) + FREE))
                pe.matmul(out_ps[0][:, 0:2 * C], same_head[:], mv_rw[:].rearrange("p a c -> p (a c)"),
                          start=True, stop=True).then_inc(head_sum, 1)
                pe.wait_ge(dev_sq, b * 1)
                pe.matmul(out_ps[0][:, 2 * C:3 * C], same_head[:], dev2[:], start=True, stop=True).then_inc(dev_sum, 1)

            def out_product(s, n):
                h, t = divmod(n, 2)
                if n == 0:
                    pe.wait_ge(head_var, s.b * 1)
                pe.wait_ge(ylo_made, known(s.nth(h + 1, 2, -NB)))
                pe.wait_ge(x2_made, known(s.nth(n - 1, TT, -NB) + FREE))
                cols = slice(t * P, (t + 1) * P)
                for g in range(C):
                    hi, lo = y_hi[:, h, g, cols], y_lo[:, h, g, cols]
                    pe.matmul(out_ps[n % 2][:], hi, w_hi[:, 3, g, :], start=(g == 0), stop=False)
                    pe.matmul(out_ps[n % 2][:], hi, w_lo[:, 3, g, :], start=False, stop=False)
                    mm = pe.matmul(out_ps[n % 2][:], lo, w_hi[:, 3, g, :], start=False, stop=(g == C - 1))
                mm.then_inc(out_summed, 1)

            def program(b, here, more, behind):
                for i in range(NB):
                    s = Step(b, i, NB)
                    ahead = here and (more or i < NB - 1)
                    if ahead:
                        turn(s, 0, 1)
                        turn(s, 1, 1)
                    if here:
                        project(s, KIND_R)
                    if behind and i == 0:
                        head_sums(b)
                    if ahead:
                        turn(s, 2, 1)
                        turn(s, 3, 1)
                    if behind:
                        for n in range(TT):
                            out_product(s, n)
                    if ahead:
                        project(s, KIND_K, 1)
                        project(s, KIND_V, 1)

            first = Step(0, 0, NB)
            pe.sem_inc(out_summed, FREE)
            pe.wait_ge(ident_made, 3)
            for n in range(TT):
                turn(first, n)
            pe.wait_ge(w_lo_made, 4 * C)
            project(first, KIND_K)
            project(first, KIND_V)
            whole(program, pe)

        @block.scalar
        def _(act):
            f = nc.scalar.activation
            act.preload_act_table_set(LOG_EXP)

            def copy_turned(s, n, ahead=0):
                act.wait_ge(x_turned, known(s.nth(n + 1, TT, ahead)))
                if n == 0:
                    act.wait_ge(shift_kept, known(s.nth(1, 1, ahead)))
                f(xT[:, :, 1 + n * P:1 + (n + 1) * P], tp_ps[n % 2][:], ACT.Copy).then_inc(xT_made, 1)

            def x_rstd(s, pair, ahead=0):
                act.wait_ge(xstat, known(s.nth(pair + 1, 2, ahead)))
                f(ln_x[:], mv_x[:, :, 1], ACT.Ln, bias=ln_eps[:]).then_inc(xlog, 1)
                act.wait_ge(xlog, known(s.nth(pair + 1, 2, ahead)))
                f(rstd_x[:], ln_x[:], ACT.Exp, scale=-0.5).then_inc(xrstd, 1)

            def mix_high(s, kind, ahead, c):
                act.wait_ge(mix_made, known(s.nth(C * kind + c + 1, 3 * C, ahead)))
                if c < C - 1:
                    act.wait_ge(chunk_used, known(s.nth((C - 1) * (kind - 1) + c + 1, 3 * (C - 1), ahead)))
                else:
                    act.wait_ge(kind_summed, known(s.nth(C * kind, 3 * C, ahead)))
                f(mix_hi[:, c, :], mixed[:, c % 2, :], ACT.Copy).then_inc(hi_made, 1)

            def copy_k(s, g, ahead=0):
                act.wait_ge(kind_summed, known(s.nth(C * KIND_K + g + 1, 3 * C, ahead)))
                act.wait_ge(gap_made, known(s.nth(g + 1, C, ahead - 1)))
                f(kk[:, g, :], acc_ps[g][:], ACT.Copy).then_inc(kind_out, 1)

            def copy_v(s, g, ahead=0):
                act.wait_ge(kind_summed, known(s.nth(C * KIND_V + g + 1, 3 * C, ahead)))
                act.wait_ge(e2v_made, known(s.nth(g + 1, C, ahead - 1)))
                f(vv[:, g, :], acc_ps[g][:], ACT.Copy).then_inc(kind_out, 1)

            def copy_r(s, g):
                act.wait_ge(kind_summed, known(s.nth(C * KIND_R + g + 1, 3 * C)))
                act.wait_ge(gated, known(s.nth(g + 1, C, -1)))
                f(sig[:, g, :], acc_ps[g][:], ACT.Sigmoid).then_inc(kind_out, 1)

            def fade(s, g):
                act.wait_ge(fade_arg, known(s.nth(g + 1, C)))
                f(A[:, g % 2, :], A[:, g % 2, :], ACT.Exp).then_inc(fade_made, 1)

            def fresh(s, g):
                act.wait_ge(fresh_arg, known(s.nth(g + 1, C)))
                f(E[:, g % 2, :], E[:, g % 2, :], ACT.Exp).then_inc(fresh_made, 1)

            def mass_log(s, g):
                act.wait_ge(mass_kept, known(s.nth(g + 1, C)))
                f(S_[:, g % 2, 1:], S_[:, g % 2, 1:], ACT.Ln, bias=eps[:]).then_inc(log_made, 1)

            def gates(s, g):
                j, n = g % 2, known(s.nth(g + 1, C))
                act.wait_ge(logm_kept, n)
                f(S_[:, j, 1:], M[:, j, 0:T], ACT.Relu, bias=bonus[:, g:g + 1], scale=-1.0).then_inc(e1_arg, 1)
                act.wait_ge(keep_arg, n)
                f(A[:, j, :], A[:, j, :], ACT.Exp).then_inc(keep_made, 1)
                act.wait_ge(add_arg, n)
                f(E[:, j, :], E[:, j, :], ACT.Exp, scale=-1.0).then_inc(add_made, 1)
                act.wait_ge(e1_arg, n)
                f(M[:, j, 0:T], M[:, j, 0:T], ACT.Relu, bias=neg_bonus[:, g:g + 1]).then_inc(e2_arg, 1)
                f(S_[:, j, 1:], S_[:, j, 1:], ACT.Exp, scale=-1.0).then_inc(e1_made, 1)
                act.wait_ge(e2_arg, n)
                f(M[:, j, 0:T], M[:, j, 0:T], ACT.Exp, scale=-1.0).then_inc(e2_made, 1)

            def inverse(s, g):
                act.wait_ge(den_made, known(s.nth(g + 1, C)))
                f(A[:, g % 2, :], A[:, g % 2, :], ACT.Ln).then_inc(den_log, 1)
                act.wait_ge(den_log, known(s.nth(g + 1, C)))
                f(A[:, g % 2, :], A[:, g % 2, :], ACT.Exp, scale=-1.0).then_inc(den_inv, 1)

            def head_rstds(b):
                act.wait_ge(head_var, b * 1)
                f(ln_h[:], var_h[:], ACT.Ln, bias=ln_eps[:]).then_inc(head_log, 1)
                act.wait_ge(head_log, b * 1)
                f(rstd_h[:], ln_h[:], ACT.Exp, scale=-0.5).then_inc(head_rstd, 1)

            def y_high(s):
                act.wait_ge(y_made, known(s.nth(C, C, -NB)))
                for h in range(2):
                    act.wait_ge(out_summed, known(s.nth(2 * h + 2, TT, -NB - 1) + FREE))
                    f(y_hi[:, h], rw[:, :, s.i * T + h * T // 2:s.i * T + (h + 1) * T // 2],
                      ACT.Copy).then_inc(yhi_made, 1)

            def program(b, here, more, behind):
                for i in range(NB):
                    s = Step(b, i, NB)
                    ahead = here and (more or i < NB - 1)
                    for g in range(C):
                        sb_, gb = groups(s, g)
                        back = sb_ is not None and (here or (i == 0 and g == 0))
                        kind, by = {0: (KIND_R, 0), 1: (None, 0), 2: (KIND_K, 1), 3: (KIND_V, 1)}[g]
                        mixing = kind is not None and (ahead if by else here)
                        if here:
                            fade(s, g)
                            fresh(s, g)
                        if mixing:
                            mix_high(s, kind, by, 0)
                        if back:
                            inverse(sb_, gb)
                        if here:
                            mass_log(s, g)
                        if ahead and g < 2:
                            x_rstd(s, g, 1)
                        if behind and g == 1 and i == 0:
                            head_rstds(b)
                            y_high(s)
                        if behind and g == 0 and i > 0:
                            y_high(s)
                        if mixing:
                            mix_high(s, kind, by, 1)
                            mix_high(s, kind, by, 2)
                        if ahead and g == 1:
                            copy_turned(s, 0, 1)
                            copy_turned(s, 1, 1)
                        if here:
                            gates(s, g)
                        if mixing:
                            mix_high(s, kind, by, 3)
                        if ahead and g == 1:
                            copy_turned(s, 2, 1)
                            copy_turned(s, 3, 1)
                        if here and g == 0:
                            for n in range(C):
                                copy_v(s, n)
                        if here and g == 1:
                            for n in range(C):
                                copy_r(s, n)
                            act.preload_act_table_set(LOG_EXP)
                        if ahead and g == 3:
                            for n in range(C):
                                copy_k(s, n, 1)

            act.wait_ge(const_loaded, 16 * 7)
            act.wait_ge(const_made, 2)
            f(neg_decay[:], decay[:], ACT.Exp).then_inc(decay_exp, 1)
            first = Step(0, 0, NB)
            for n in range(4):
                act.wait_ge(w_loaded, 16 * (n + 1))
                for c in range(C):
                    f(w_hi[:, n, c, :], stage[:, c, :], ACT.Copy).then_inc(w_hi_made, 1)
                if n == 0:
                    for pair in range(2):
                        x_rstd(first, pair)
                        copy_turned(first, 2 * pair)
                        copy_turned(first, 2 * pair + 1)
            for c in range(C):
                mix_high(first, KIND_K, 0, c)
            for g in range(C):
                copy_k(first, g)
            for c in range(C):
                mix_high(first, KIND_V, 0, c)
            whole(program, act)

        @block.vector
        def _(dve):
            v = nc.vector
            v.memset(eps[:], EPS).then_inc(const_made, 1)
            v.memset(ln_eps[:], LN_EPS).then_inc(const_made, 1)
            dve.sem_inc(x2_made, FREE)

            def x_stats(s, pair, ahead=0):
                for n in (2 * pair, 2 * pair + 1):
                    dve.wait_ge(x_loaded[n % 2], known(s.nth(n // 2 + 1, TT // 2, ahead) * 16))
                    v.bn_stats(bn_x[:, n % 2, :], xin[:, n % 2, :]).then_inc(xbn, 1)
                for n in (2 * pair, 2 * pair + 1):
                    dve.wait_ge(xbn, known(s.nth(n + 1, TT, ahead)))
                    dve.sem_inc(passed, 1)
                    ins = v.bn_aggr(mv_x[:, n % 2, :], bn_x[:, n % 2, :])
                ins.then_inc(xstat, 1)

            def x_norm(s, pair, ahead=0):
                dve.wait_ge(xrstd, known(s.nth(pair + 1, 2, ahead)))
                for n in (2 * pair, 2 * pair + 1):
                    v.tensor_scalar(xin[:, n % 2, :], xin[:, n % 2, :], mv_x[:, n % 2, 0:1], rstd_x[:, n % 2:n % 2 + 1],
                                    ALU.subtract, ALU.mult).then_inc(xnormed, 1)

            def keep_shift(s, ahead=0):
                dve.wait_ge(mix_made, known(s.nth(0, 3 * C, ahead)))
                if (s.i + ahead) % NB == 0:
                    v.memset(xT[:, :, 0:1], 0.0).then_inc(shift_kept, 1)
                else:
                    v.tensor_copy(xT[:, :, 0:1], xT[:, :, T:T + 1]).then_inc(shift_kept, 1)

            def difference(s, ahead=0):
                dve.wait_ge(xT_made, known(s.nth(TT, TT, ahead)))
                for c in range(C):
                    v.tensor_tensor(xd[:, c, :], xT[:, c, 1:], xT[:, c, 0:T], ALU.subtract).then_inc(diff_made, 1)

            def mix(s, kind, ahead, c):
                dve.wait_ge(diff_made, known(s.nth(c + 1, C, ahead)))
                dve.wait_ge(lo_made, known(s.nth(C * kind + c - 1, 3 * C, ahead)))
                v.scalar_tensor_tensor(mixed[:, c % 2, :], xd[:, c, :], mixc[:, kind, c:c + 1], xT[:, c, 0:T],
                                       ALU.mult, ALU.add).then_inc(mix_made, 1)

            def start_front():
                for tile, value in ((peak_c, LOWEST), (logm_c, LOWEST), (mass_c, 1.0)):
                    ins = v.memset(tile[:], value)
                ins.then_inc(start_set, 1)

            def peak(s, g):
                j = g % 2
                if s.i == 0 and g == 0:
                    start_front()
                    dve.wait_ge(start_set, s.b + 1)
                dve.wait_ge(num_made, known(s.nth(g - 1, C)))
                v.tensor_copy(M[:, j, 0:1], peak_c[:, g:g + 1]).then_inc(peak_in, 1)
                dve.wait_ge(kind_out, known(s.nth(C * KIND_K + g + 1, 3 * C)))
                v.tensor_tensor_scan(M[:, j, 1:], decay[:, g:g + 1].to_broadcast([P, T]), kk[:, g, :],
                                     peak_c[:, g:g + 1], ALU.add, ALU.max).then_inc(peak_made, 1)

            def fade(s, g):
                j = g % 2
                dve.wait_ge(peak_made, known(s.nth(g + 1, C)))
                dve.wait_ge(rw_made, known(s.nth(g - 1, C)))
                v.scalar_tensor_tensor(A[:, j, :], M[:, j, 0:T], decay[:, g:g + 1], M[:, j, 1:],
                                       ALU.add, ALU.subtract).then_inc(fade_arg, 1)
                v.tensor_copy(peak_c[:, g:g + 1], M[:, j, T:T + 1]).then_inc(peak_kept, 1)

            def mass(s, g):
                j = g % 2
                dve.wait_ge(fresh_made, known(s.nth(g + 1, C)))
                v.tensor_tensor_scan(S_[:, j, 1:], A[:, j, :], E[:, j, :], mass_c[:, g:g + 1],
                                     ALU.mult, ALU.add).then_inc(mass_made, 1)
                v.tensor_copy(S_[:, j, 0:1], logm_c[:, g:g + 1]).then_inc(logm_in, 1)
                dve.wait_ge(mass_made, known(s.nth(g + 1, C)))
                v.tensor_copy(mass_c[:, g:g + 1], S_[:, j, T:T + 1]).then_inc(mass_kept, 1)

            def gap(s, g):
                j = g % 2
                dve.wait_ge(logm_made, known(s.nth(g + 1, C)))
                dve.wait_ge(peak_kept, known(s.nth(g + 1, C)))
                v.tensor_tensor(M[:, j, 0:T], S_[:, j, 0:T], kk[:, g, :], ALU.subtract).then_inc(gap_made, 1)
                v.tensor_copy(logm_c[:, g:g + 1], S_[:, j, T:T + 1]).then_inc(logm_kept, 1)
                dve.wait_ge(gap_made, known(s.nth(g + 1, C)))
                v.tensor_scalar(A[:, j, :], M[:, j, 0:T], decay[:, g:g + 1], 0.0, ALU.add, ALU.min).then_inc(keep_arg, 1)
                v.tensor_scalar(E[:, j, :], M[:, j, 0:T], decay[:, g:g + 1], 0.0, ALU.add, ALU.max).then_inc(add_arg, 1)

            def add_v(s, g):
                j = g % 2
                dve.wait_ge(kind_out, known(s.nth(C * KIND_V + g + 1, 3 * C)))
                dve.wait_ge(add_made, known(s.nth(g + 1, C)))
                v.tensor_tensor(E[:, j, :], E[:, j, :], vv[:, g, :], ALU.mult).then_inc(addv_made, 1)

            def accumulate(s, g):
                j = g % 2
                dve.wait_ge(e1a_made, known(s.nth(g - 1, C)))
                v.tensor_copy(acc[:, j, 0:1], acc_c[:, g:g + 1]).then_inc(acc_in, 1)
                dve.wait_ge(addv_made, known(s.nth(g + 1, C)))
                v.tensor_tensor_scan(acc[:, j, 1:], A[:, j, :], E[:, j, :], acc_c[:, g:g + 1],
                                     ALU.mult, ALU.add).then_inc(acc_made, 1)

            def denominator(s, g):
                j = g % 2
                dve.wait_ge(e2_made, known(s.nth(g + 1, C)))
                dve.wait_ge(acc_made, known(s.nth(g + 1, C)))
                v.scalar_tensor_tensor(A[:, j, :], M[:, j, 0:T], EPS, S_[:, j, 1:],
                                       ALU.add, ALU.add).then_inc(den_made, 1)
                v.tensor_copy(acc_c[:, g:g + 1], acc[:, j, T:T + 1]).then_inc(acc_kept, 1)

            def numerator(s, g):
                j = g % 2
                dve.wait_ge(e2v_made, known(s.nth(g + 1, C)))
                v.tensor_tensor(S_[:, j, 1:], S_[:, j, 1:], M[:, j, 0:T], ALU.add).then_inc(num_made, 1)

            def result(s, g):
                j, rows = g % 2, slice(s.i % NB * T, (s.i % NB + 1) * T)
                dve.wait_ge(gated, known(s.nth(g + 1, C)))
                dve.wait_ge(num_made, known(s.nth(g + 1, C)))
                if g == 0:
                    dve.wait_ge(ylo_made, known(s.nth(2, 2, -NB)))
                v.tensor_tensor(rw[:, g, rows], S_[:, j, 1:], A[:, j, :], ALU.mult).then_inc(rw_made, 1)
                dve.wait_ge(rw_made, known(s.nth(g + 1, C)))
                v.bn_stats(bn_rw[:, g, s.i % NB, :], rw[:, g, rows]).then_inc(rw_bn, 1)

            def channel_stats(b):
                dve.wait_ge(rw_bn, b * (NB * C))
                dve.sem_inc(passed, 1)
                for g in range(C):
                    ins = v.bn_aggr(mv_rw[:, :, g], bn_rw[:, g].rearrange("p n k -> p (n k)"))
                ins.then_inc(chan_stats, 1)

            def head_deviation(b):
                dve.wait_ge(head_sum, b * 1)
                v.tensor_copy(mv_head[:].rearrange("p a c -> p (a c)"), out_ps[0][:, 0:2 * C]).then_inc(head_copied, 1)
                dve.wait_ge(head_copied, b * 1)
                v.tensor_tensor(dev[:], mv_rw[:, 0, :], mv_head[:, 0, :], ALU.subtract).then_inc(dev_made, 1)
                dve.wait_ge(dev_made, b * 1)
                v.tensor_tensor(dev2[:], dev[:], dev[:], ALU.mult).then_inc(dev_sq, 1)

            def head_variance(b):
                dve.wait_ge(dev_sum, b * 1)
                v.tensor_tensor(var_h[:], out_ps[0][:, 2 * C:3 * C], mv_head[:, 1, :], ALU.add).then_inc(head_var, 1)

            def head_affine(b):
                dve.wait_ge(head_rstd, b * 1)
                v.tensor_tensor(scale_h[:], rstd_h[:], gamma[:], ALU.mult).then_inc(scale_made, 1)
                dve.wait_ge(scale_made, b * 1)
                v.tensor_tensor(mean_s[:], mv_head[:, 0, :], scale_h[:], ALU.mult).then_inc(shift_mul, 1)
                dve.wait_ge(shift_mul, b * 1)
                v.tensor_tensor(shift_h[:], beta[:], mean_s[:], ALU.subtract).then_inc(shift_made, 1)
                dve.wait_ge(shift_made, b * 1)

            def normed(s):
                for g in range(C):
                    part = rw[:, g, s.i * T:(s.i + 1) * T]
                    v.tensor_scalar(part, part, scale_h[:, g:g + 1], shift_h[:, g:g + 1],
                                    ALU.mult, ALU.add).then_inc(y_made, 1)

            def residual(s, n):
                dve.wait_ge(xres_loaded[n % 2], known(s.nth(n // 2 + 1, TT // 2, -NB) * 16))
                dve.wait_ge(x2_stored[n % 2], known((s.nth(n // 2, TT // 2, -NB) + FREE) * 16))
                dve.wait_ge(out_summed, known(s.nth(n + 1, TT, -NB) + FREE))
                v.tensor_tensor(xout[:, n % 2, :], out_ps[n % 2][:], xres[:, n % 2, :], ALU.add).then_inc(x2_made, 1)

            def program(b, here, more, behind):
                for i in range(NB):
                    s = Step(b, i, NB)
                    ahead = here and (more or i < NB - 1)
                    for g in range(C):
                        sb_, gb = groups(s, g)
                        back = sb_ is not None and (here or (i == 0 and g == 0))
                        kind, by = {0: (KIND_R, 0), 1: (None, 0), 2: (KIND_K, 1), 3: (KIND_V, 1)}[g]
                        mixing = kind is not None and (ahead if by else here)
                        if behind and g == 0 and i > 0:
                            normed(s)
                        if here:
                            peak(s, g)
                        if back:
                            add_v(sb_, gb)
                        if here:
                            fade(s, g)
                        if back:
                            accumulate(sb_, gb)
                        if ahead and g == 2:
                            difference(s, 1)
                        if mixing:
                            mix(s, kind, by, 0)
                        if back:
                            denominator(sb_, gb)
                        if ahead and g < 2:
                            x_stats(s, g, 1)
                        if here:
                            mass(s, g)
                        if behind and g == 1 and i == 0:
                            head_deviation(b)
                        if mixing:
                            mix(s, kind, by, 1)
                            mix(s, kind, by, 2)
                        if ahead and g < 2:
                            x_norm(s, g, 1)
                        if behind and g >= 2:
                            residual(s, 2 * g - 4)
                        if back:
                            numerator(sb_, gb)
                        if behind and g == 1 and i == 0:
                            head_variance(b)
                        if here:
                            gap(s, g)
                        if behind and g == 1 and i == 0:
                            head_affine(b)
                            normed(s)
                        if mixing:
                            mix(s, kind, by, 3)
                        if ahead and g == 0:
                            keep_shift(s, 1)
                        if back:
                            result(sb_, gb)
                        if behind and g >= 2:
                            residual(s, 2 * g - 3)
                        if i == 0 and g == 0:
                            if behind:
                                channel_stats(b)
                            v.memset(acc_c[:], 0.0).then_inc(acc_start, 1)
                            dve.wait_ge(acc_start, b + 1)

            dve.wait_ge(decay_exp, 1)
            v.tensor_scalar(decay[:], neg_decay[:], -1.0, None, ALU.mult)
            v.tensor_scalar(neg_bonus[:], bonus[:], -1.0, None, ALU.mult).then_inc(bonus_neg, 1)
            dve.wait_ge(bonus_neg, 1)
            first = Step(0, 0, NB)
            keep_shift(first)
            for pair in range(2):
                x_stats(first, pair)
                x_norm(first, pair)
            difference(first)
            for kind in (KIND_K, KIND_V):
                for c in range(C):
                    mix(first, kind, 0, c)
            whole(program, dve)


def feed_forward(nc, sem, x2, w1, w3, w2, out, B, S):
    E, D, F = w1.shape
    C = D // P
    FC = F // P
    CAP = S // E
    N = B * CAP
    NT = N // P
    TB = CAP // P
    NH = N // T
    R = 3
    LN_AT = (0, 1, 3, 4)

    with ExitStack() as ctx:
        def sb(name, shape, dt=F32):
            return ctx.enter_context(nc.sbuf_tensor(name, shape, dt))

        def psum(name, shape):
            return ctx.enter_context(nc.psum_tensor(name, shape, F32))

        ident = sb("ident2", [P, P])
        ln_eps = sb("ln_eps2", [P, 1])
        w13_in = sb("w13_in", [P, 2, 2, C, P])
        w13_hi = sb("w13_hi", [P, R, 2, C, P], F32R)
        w13_lo = sb("w13_lo", [P, R, 2, C, P], F32R)
        w2_in = sb("w2_in", [P, 2, D])
        w2_hi = sb("w2_hi", [P, FC, D], F32R)
        w2_lo = sb("w2_lo", [P, FC, D], F32R)
        xt = sb("xt", [P, 2, TB, D])
        bn = sb("bn", [P, TB, 6])
        mv = sb("mv", [P, TB, 2])
        lnv = sb("lnv", [P, TB])
        rstd = sb("rstd", [P, TB])
        xT_hi = sb("xT_hi", [P, C, N], F32R)
        xT_lo = sb("xT_lo", [P, C, N], F32R)
        gated = sb("gated2", [P, 2, T])
        hid = sb("hid", [P, FC, N])
        hid_hi = sb("hid_hi", [P, 2, FC, P], F32R)
        hid_lo = sb("hid_lo", [P, 2, FC, P], F32R)
        xres = sb("xres2", [P, 2, D])
        xout = sb("xout2", [P, 2, D])

        gate_ps = [psum(f"gate_ps{n}", [P, T]) for n in range(2)]
        up_ps = [psum(f"up_ps{n}", [P, T]) for n in range(2)]
        turn_ps = [psum(f"turn_ps{n}", [P, C, P]) for n in range(2)]
        down_ps = [psum(f"down_ps{n}", [P, D]) for n in range(2)]

        passed = sem("passed2")
        w13_loaded, w2_loaded, xt_loaded, res_loaded, out_stored = (
            [sem(f"{name}{n}") for n in range(2)]
            for name in ("w13_loaded", "w2_loaded", "xt_loaded", "res_loaded", "out_stored"))
        (id_zero, id_made, eps_made, w13_high, w13_low, w2_high, w2_low) = map(
            sem, ("id_zero", "id_made", "eps_made", "w13_high", "w13_low", "w2_high", "w2_low"))
        (bn_done, stat_done, log_done, rstd_done, norm_done, turned, xT_high, xT_low) = map(
            sem, ("bn_done", "stat_done", "log_done", "rstd_done", "norm_done", "turned", "xT_high", "xT_low"))
        (gate_summed, up_summed, silu_made, hid_made, hid_high, hid_low, down_summed, out_made) = map(
            sem, ("gate_summed", "up_summed", "silu_made", "hid_made", "hid_high", "hid_low", "down_summed", "out_made"))

        def whole(program, eng):
            with eng.Fori(0, E - 1) as e:
                program(e, True)
            program(E - 1, False)

        def ring(f, slots):
            f %= FC
            if f >= slots:
                return f - slots
            return max(n for n in range(FC) if n % slots == f % slots) - FC

        def nth_load(e, f):
            return e * len(range(f % 2, FC, 2)) + (f // 2 + 1)

        def tokens(t, e, n, count=1):
            m, h = divmod(n, TB)
            tiles = t.rearrange("(n p) d -> n p d", p=P)
            return tiles[bass.ds(e * TB + (m * (S // P) + h), count)].rearrange("n p d -> p n d")

        block = ctx.enter_context(nc.Block())

        @block.sync
        def _(sp):
            for stored in out_stored:
                sp.sem_inc(stored, 16 * FREE)

            def load_w13(e, f):
                prev = ring(f, 2)
                e, f = e + f // FC, f % FC
                sp.wait_ge(w13_low, known((e * FC + (prev + 1)) * 2))
                for n, w in enumerate((w1, w3)):
                    src = w.rearrange("e (c p) f -> e p c f", p=P)[bass.ds(e, 1), :, :, f * P:(f + 1) * P]
                    sp.dma_start(w13_in[:, f % 2, n], src.rearrange("o p c f -> (o p) c f")).then_inc(w13_loaded[f % 2], 16)

            def load_w2(e, f):
                prev = ring(f, 2)
                e, f = e + f // FC, f % FC
                sp.wait_ge(w2_low, known(e * FC + (prev + 1)))
                src = w2[bass.ds(e, 1), f * P:(f + 1) * P, :]
                sp.dma_start(w2_in[:, f % 2], src.rearrange("o p d -> (o p) d")).then_inc(w2_loaded[f % 2], 16)

            def load_xt(e, m):
                sp.wait_ge(turned, known(e * NT + (m - 1) * TB))
                sp.dma_start(xt[:, m % 2], tokens(x2, e, m * TB, TB)).then_inc(xt_loaded[m % 2], 16)

            load_xt(0, 0)
            load_xt(0, 1)
            load_w13(0, 0)
            load_w13(0, 1)
            load_xt(0, 2)
            load_xt(0, 3)
            load_w2(0, 0)
            load_w2(0, 1)
            load_w13(0, 2)

            def program(e, more):
                for f in range(FC):
                    if more or f + 3 < FC:
                        load_w13(e, f + 3)
                    if more or f + 2 < FC:
                        load_w2(e, f + 2)
                for n in range(NT + 2):
                    if n < NT:
                        sp.wait_ge(out_made, known(e * NT + (n - 1 + FREE)))
                        sp.dma_start(xres[:, n % 2:n % 2 + 1], tokens(x2, e, n)).then_inc(res_loaded[n % 2], 16)
                    if n < B and more:
                        load_xt(e + 1, n)
                    if n >= 2:
                        sp.wait_ge(out_made, known(e * NT + (n - 1 + FREE)))
                        sp.dma_start(tokens(out, e, n - 2), xout[:, n % 2:n % 2 + 1]).then_inc(out_stored[n % 2], 16)

            whole(program, sp)
            for stored in out_stored:
                sp.wait_ge(stored, 16 * (E * NT // 2 + FREE))

        @block.gpsimd
        def _(pool):
            g_ = nc.gpsimd
            g_.memset(ident[:], 0.0).then_inc(id_zero, 1)
            pool.wait_ge(id_zero, 1)
            g_.affine_select(out=ident[:], in_=ident[:], compare_op=ALU.not_equal, fill=1.0, base=0,
                             pattern=[[-1, P]], channel_multiplier=1).then_inc(id_made, 1)

            def low_w13(e, f):
                e, f = e + f // FC, f % FC
                pool.wait_ge(w13_high, known((e * FC + f + 1) * 2))
                for n in range(2):
                    g_.tensor_tensor(w13_lo[:, f % R, n], w13_in[:, f % 2, n], w13_hi[:, f % R, n].bitcast(F32),
                                     ALU.subtract).then_inc(w13_low, 1)

            def low_w2(e, f):
                pool.wait_ge(w2_high, known(e * FC + (f + 1)))
                g_.tensor_tensor(w2_lo[:, f], w2_in[:, f % 2], w2_hi[:, f].bitcast(F32), ALU.subtract).then_inc(w2_low, 1)

            low_w13(0, 0)
            low_w13(0, 1)

            def program(e, more):
                for f in range(FC):
                    if more or f + 2 < FC:
                        low_w13(e, f + 2)
                    low_w2(e, f)

            whole(program, pool)

        @block.tensor
        def _(pe):
            pe.sem_inc(up_summed, FREE * NH)
            pe.sem_inc(down_summed, FREE)

            def turn(e, m):
                for n in range(m * TB, (m + 1) * TB):
                    pe.wait_ge(norm_done, known(e * NT + (n + 1)))
                    pe.wait_ge(xT_low, known(e * NT + (n - 1)))
                    for c in range(C):
                        mm = pe.transpose(turn_ps[n % 2][:, c, :], xt[:, m % 2, n % TB, c * P:(c + 1) * P], ident[:])
                    mm.then_inc(turned, 1)

            def products(bank, w, f, cols):
                for c in range(C):
                    hi, lo = w13_hi[:, f % R, w, c, :], w13_lo[:, f % R, w, c, :]
                    pe.matmul(bank[:], hi, xT_hi[:, c, cols], start=(c == 0), stop=False)
                    pe.matmul(bank[:], hi, xT_lo[:, c, cols], start=False, stop=False)
                    mm = pe.matmul(bank[:], lo, xT_hi[:, c, cols], start=False, stop=(c == C - 1))
                return mm

            def gate_up(e):
                pe.wait_ge(xT_low, known(e * NT + NT))
                for f in range(FC):
                    pe.wait_ge(w13_low, known((e * FC + (f + 1)) * 2))
                    for h in range(NH):
                        k = NH * f + h
                        cols = slice(h * T, (h + 1) * T)
                        pe.wait_ge(silu_made, known(e * (NH * FC) + (k - 1 + FREE)))
                        products(gate_ps[k % 2], 0, f, cols).then_inc(gate_summed, 1)
                        pe.wait_ge(hid_made, known(e * (NH * FC) + (k - 1 + FREE)))
                        mm = products(up_ps[k % 2], 1, f, cols)
                        mm.then_inc(up_summed, 1)

            def down(e, n):
                if n == 0:
                    pe.wait_ge(w2_low, known(e * FC + FC))
                pe.wait_ge(hid_low, known(e * NT + (n + 1 + FREE)))
                pe.wait_ge(out_made, known(e * NT + (n - 1 + FREE)))
                for f in range(FC):
                    hi, lo = hid_hi[:, n % 2, f, :], hid_lo[:, n % 2, f, :]
                    pe.matmul(down_ps[n % 2][:], hi, w2_hi[:, f, :], start=(f == 0), stop=False)
                    pe.matmul(down_ps[n % 2][:], hi, w2_lo[:, f, :], start=False, stop=False)
                    mm = pe.matmul(down_ps[n % 2][:], lo, w2_hi[:, f, :], start=False, stop=(f == FC - 1))
                mm.then_inc(down_summed, 1)

            pe.wait_ge(id_made, 1)
            for m in range(B):
                turn(0, m)

            def program(e, more):
                gate_up(e)
                for n in range(NT):
                    down(e, n)
                    if more and n in LN_AT:
                        turn(e + 1, LN_AT.index(n))

            whole(program, pe)

        @block.scalar
        def _(act):
            f_ = nc.scalar.activation
            act.sem_inc(silu_made, FREE)

            def high_w13(e, f):
                prev = ring(f, R)
                e, f = e + f // FC, f % FC
                act.wait_ge(w13_loaded[f % 2], known(nth_load(e, f) * 32))
                act.wait_ge(up_summed, known((e * FC + (prev + 1)) * NH + FREE * NH))
                for n in range(2):
                    f_(w13_hi[:, f % R, n], w13_in[:, f % 2, n], ACT.Copy).then_inc(w13_high, 1)

            def high_w2(e, f):
                act.wait_ge(w2_loaded[f % 2], known(nth_load(e, f) * 16))
                if f == 0:
                    act.wait_ge(down_summed, known(e * NT + FREE))
                f_(w2_hi[:, f], w2_in[:, f % 2], ACT.Copy).then_inc(w2_high, 1)

            def x_rstd(e, m):
                act.wait_ge(stat_done, known(e * B + (m + 1)))
                f_(lnv[:], mv[:, :, 1], ACT.Ln, bias=ln_eps[:]).then_inc(log_done, 1)
                act.wait_ge(log_done, known(e * B + (m + 1)))
                f_(rstd[:], lnv[:], ACT.Exp, scale=-0.5).then_inc(rstd_done, 1)

            def turned_high(e, m):
                for n in range(m * TB, (m + 1) * TB):
                    act.wait_ge(turned, known(e * NT + (n + 1)))
                    f_(xT_hi[:, :, n * P:(n + 1) * P], turn_ps[n % 2][:], ACT.Copy).then_inc(xT_high, 1)

            def silu(e, k):
                act.wait_ge(gate_summed, known(e * (NH * FC) + (k + 1)))
                act.wait_ge(hid_made, known(e * (NH * FC) + (k - 1 + FREE)))
                f_(gated[:, k % 2], gate_ps[k % 2][:], ACT.Silu).then_inc(silu_made, 1)

            def hidden_high(e, n):
                if n == 0:
                    act.wait_ge(hid_made, known(e * (NH * FC) + (NH * FC + FREE)))
                act.wait_ge(down_summed, known(e * NT + (n - 1 + FREE)))
                f_(hid_hi[:, n % 2], hid[:, :, n * P:(n + 1) * P], ACT.Copy).then_inc(hid_high, 1)

            act.preload_act_table_set(LOG_EXP)
            act.wait_ge(eps_made, 1)
            for m in range(B):
                x_rstd(0, m)
                turned_high(0, m)
                if m < 2:
                    high_w13(0, m)

            def program(e, more):
                for f in range(FC):
                    for h in range(NH):
                        silu(e, NH * f + h)
                    if more or f + 2 < FC:
                        high_w13(e, f + 2)
                    high_w2(e, f)
                act.preload_act_table_set(LOG_EXP)
                for n in range(NT):
                    hidden_high(e, n)
                    if more and n - 2 in LN_AT:
                        turned_high(e + 1, LN_AT.index(n - 2))
                    if more and n in LN_AT:
                        x_rstd(e + 1, LN_AT.index(n))

            whole(program, act)

        @block.vector
        def _(dve):
            v = nc.vector
            v.memset(ln_eps[:], LN_EPS).then_inc(eps_made, 1)
            dve.sem_inc(hid_made, FREE)
            dve.sem_inc(hid_low, FREE)
            dve.sem_inc(out_made, FREE)

            def x_stats(e, m):
                dve.wait_ge(xt_loaded[m % 2], known((e * (B // 2) + (m // 2 + 1)) * 16))
                for t in range(TB):
                    v.bn_stats(bn[:, t], xt[:, m % 2, t]).then_inc(bn_done, 1)
                for t in range(TB):
                    dve.wait_ge(bn_done, e * NT + (m * TB + t + 1))
                    dve.sem_inc(passed, 1)
                    ins = v.bn_aggr(mv[:, t], bn[:, t])
                ins.then_inc(stat_done, 1)

            def x_norm(e, m):
                dve.wait_ge(rstd_done, known(e * B + (m + 1)))
                for t in range(TB):
                    v.tensor_scalar(xt[:, m % 2, t], xt[:, m % 2, t], mv[:, t, 0:1], rstd[:, t:t + 1],
                                    ALU.subtract, ALU.mult).then_inc(norm_done, 1)

            def turned_low(e, m):
                for n in range(m * TB, (m + 1) * TB):
                    cols = slice(n * P, (n + 1) * P)
                    dve.wait_ge(xT_high, known(e * NT + (n + 1)))
                    v.tensor_tensor(xT_lo[:, :, cols], turn_ps[n % 2][:], xT_hi[:, :, cols].bitcast(F32),
                                    ALU.subtract).then_inc(xT_low, 1)

            def hidden(e, k):
                f, h = divmod(k, NH)
                dve.wait_ge(silu_made, known(e * (NH * FC) + (k + 1 + FREE)))
                dve.wait_ge(up_summed, known(e * (NH * FC) + (k + 1 + NH * FREE)))
                if k == 0:
                    dve.wait_ge(hid_low, known(e * NT + FREE))
                v.tensor_tensor(hid[:, f, h * T:(h + 1) * T], up_ps[k % 2][:], gated[:, k % 2],
                                ALU.mult).then_inc(hid_made, 1)

            def hidden_low(e, n):
                dve.wait_ge(hid_high, known(e * NT + (n + 1)))
                v.tensor_tensor(hid_lo[:, n % 2], hid[:, :, n * P:(n + 1) * P], hid_hi[:, n % 2].bitcast(F32),
                                ALU.subtract).then_inc(hid_low, 1)

            def residual(e, n):
                dve.wait_ge(down_summed, known(e * NT + (n + 1 + FREE)))
                dve.wait_ge(res_loaded[n % 2], known((e * (NT // 2) + (n // 2 + 1)) * 16))
                dve.wait_ge(out_stored[n % 2], known((e * (NT // 2) + (n // 2 + FREE)) * 16))
                v.tensor_tensor(xout[:, n % 2], down_ps[n % 2][:], xres[:, n % 2], ALU.add).then_inc(out_made, 1)

            for m in range(B):
                x_stats(0, m)
                x_norm(0, m)
                turned_low(0, m)

            def program(e, more):
                for k in range(NH * FC):
                    hidden(e, k)
                for n in range(NT):
                    hidden_low(e, n)
                    if n >= 2:
                        residual(e, n - 2)
                    if more and n - 2 in LN_AT:
                        turned_low(e + 1, LN_AT.index(n - 2))
                    if more and n in LN_AT:
                        x_stats(e + 1, LN_AT.index(n))
                        x_norm(e + 1, LN_AT.index(n))
                residual(e, NT - 2)
                residual(e, NT - 1)

            whole(program, dve)


def kernel(**inputs):
    import numpy as np
    import concourse.bacc as bacc
    from concourse.bass_utils import run_bass_kernel_spmd

    nc = bacc.Bacc("TRN2", target_bir_lowering=False, num_devices=1)
    arrays, args = {}, {}

    def give(name, array):
        array = np.ascontiguousarray(array)
        arrays[name] = array
        args[name] = nc.dram_tensor(name, array.shape, mybir.dt.from_np(array.dtype), kind="ExternalInput").ap()

    x = np.asarray(inputs["L0_attn_x"])
    B, S, D = x.shape
    give("x", x)
    for kind in "rkv":
        give("mix_" + kind, np.asarray(inputs["L0_attn_time_mix_" + kind]).reshape(D))
    for kind in "rkvo":
        give("wT_" + kind, np.asarray(inputs["L0_attn_W_" + kind]).T)
    for name in ("time_decay", "time_first", "ln_gamma", "ln_beta"):
        give(name, np.asarray(inputs["L0_attn_" + name]).reshape(D))
    for name in ("w1", "w3", "w2"):
        give(name, inputs["L0_ffn_" + name])
    out = nc.dram_tensor("out", (B * S, D), F32, kind="ExternalOutput").ap()
    x2 = nc.dram_tensor("x2", (B * S, D), F32, kind="Internal").ap()
    with ExitStack() as ctx:
        def sem(name):
            return ctx.enter_context(nc.semaphore(name))

        time_mixing(nc, sem, args["x"], [args["mix_" + k] for k in "kvr"], [args["wT_" + k] for k in "kvro"],
                    args["time_decay"], args["time_first"], args["ln_gamma"], args["ln_beta"], x2)
        feed_forward(nc, sem, x2, args["w1"], args["w3"], args["w2"], out, B, S)
    result = run_bass_kernel_spmd(nc, [arrays], core_ids=[0]).results[0]["out"]
    return result.reshape(B, S, D)
```

```python
from contextlib import ExitStack

import concourse.bass as bass
from concourse import mybir

ALU = mybir.AluOpType
ACT = mybir.ActivationFunctionType
F32 = mybir.dt.float32
F32R = mybir.dt.float32r

P = 128
T = 512
EPS = 1e-8
LN_EPS = 1e-5
LOWEST = -1e38
LOG_EXP = "natural_log_exp_and_others"
KIND_K, KIND_V, KIND_R = range(3)


def known(count):
    return max(count, 0) if isinstance(count, int) else count


FREE = 4


class Step:

    def __init__(self, b, i, per_batch):
        self.b, self.i, self.per_batch = b, i, per_batch

    def nth(self, n, of, ahead=0):
        return self.b * (self.per_batch * of) + ((self.i + ahead) * of + n)


def time_mixing(nc, sem, x, mix_in, wT_in, decay_in, first_in, gamma_in, beta_in, x2):
    B, S, D = x.shape
    C = D // P
    HD = 32
    NB = S // T
    TT = T // P
    MIX = C - 1

    with ExitStack() as ctx:
        def sb(name, shape, dt=F32):
            return ctx.enter_context(nc.sbuf_tensor(name, shape, dt))

        def psum(name, shape):
            return ctx.enter_context(nc.psum_tensor(name, shape, F32))

        w_hi = sb("w_hi", [P, 4, C, D], F32R)
        w_lo = sb("w_lo", [P, 4, C, D], F32R)
        ident = sb("ident", [P, P])
        same_head = sb("same_head", [P, P])
        eps = sb("eps", [P, 1])
        ln_eps = sb("ln_eps", [P, 1])
        mixc = sb("mixc", [P, 3, C])
        decay = sb("decay", [P, C])
        neg_decay = sb("neg_decay", [P, C])
        bonus = sb("bonus", [P, C])
        neg_bonus = sb("neg_bonus", [P, C])
        gamma = sb("gamma", [P, C])
        beta = sb("beta", [P, C])
        xin = sb("xin", [P, 2, D])
        bn_x = sb("bn_x", [P, 2, 6])
        mv_x = sb("mv_x", [P, 2, 2])
        ln_x = sb("ln_x", [P, 2])
        rstd_x = sb("rstd_x", [P, 2])
        xT = sb("xT", [P, C, 1 + T])
        xd = sb("xd", [P, C, T])
        mixed = sb("mixed", [P, MIX, T])
        mix_hi = sb("mix_hi", [P, C, T], F32R)
        mix_lo = sb("mix_lo", [P, C, T], F32R)
        kk = sb("kk", [P, C, T])
        vv = sb("vv", [P, C, T])
        sig = sb("sig", [P, C, T])
        M = sb("M", [P, 2, 1 + T])
        A = sb("A", [P, 2, T])
        E = sb("E", [P, 2, T])
        S_ = sb("S_", [P, 2, 1 + T])
        acc = sb("acc", [P, 2, 1 + T])
        peak_c = sb("peak_c", [P, C])
        mass_c = sb("mass_c", [P, C])
        logm_c = sb("logm_c", [P, C])
        acc_c = sb("acc_c", [P, C])
        rw = sb("rw", [P, C, S])
        bn_rw = sb("bn_rw", [P, C, NB, 6])
        mv_rw = sb("mv_rw", [P, 2, C])
        mv_head = sb("mv_head", [P, 2, C])
        dev = sb("dev", [P, C])
        dev2 = sb("dev2", [P, C])
        var_h = sb("var_h", [P, C])
        ln_h = sb("ln_h", [P, C])
        rstd_h = sb("rstd_h", [P, C])
        scale_h = sb("scale_h", [P, C])
        mean_s = sb("mean_s", [P, C])
        shift_h = sb("shift_h", [P, C])
        y = sb("y", [P, C, T])
        y_hi = sb("y_hi", [P, 2, C, P], F32R)
        y_lo = sb("y_lo", [P, 2, C, P], F32R)
        xres = sb("xres", [P, 2, D])
        xout = sb("xout", [P, 1, D])

        acc_ps = [psum(f"acc_ps{g}", [P, T]) for g in range(C)]
        tp_ps = [psum(f"tp_ps{n}", [P, C, P]) for n in range(2)]
        out_ps = [psum(f"out_ps{n}", [P, D]) for n in range(2)]

        passed = sem("passed")
        const_loaded = sem("const_loaded")
        w_loaded = [sem(f"w_loaded{n}") for n in range(4)]
        acc_start = sem("acc_start")
        x_loaded, xres_loaded = ([sem(f"{name}{n}") for n in range(2)] for name in ("x_loaded", "xres_loaded"))
        x2_stored = sem("x2_stored")
        (ident_zero, ident_made, w_hi_made, w_lo_kr, w_lo_vo, decay_exp, const_made, bonus_neg) = map(
            sem, ("ident_zero", "ident_made", "w_hi_made", "w_lo_kr", "w_lo_vo", "decay_exp", "const_made", "bonus_neg"))
        (xbn, xstat, xlog, xrstd, xnormed, x_turned, shift_kept, xT_made, diff_made) = map(
            sem, ("xbn", "xstat", "xlog", "xrstd", "xnormed", "x_turned", "shift_kept", "xT_made", "diff_made"))
        (mix_made, hi_made, lo_made, chunk_used, kind_summed, kind_out) = map(
            sem, ("mix_made", "hi_made", "lo_made", "chunk_used", "kind_summed", "kind_out"))
        (start_set, peak_in, peak_made, peak_kept, fade_arg, fade_made, fresh_arg, fresh_made,
         mass_made, mass_kept, log_made, logm_in, logm_made, logm_kept, gap_made) = map(
            sem, ("start_set", "peak_in", "peak_made", "peak_kept", "fade_arg", "fade_made", "fresh_arg", "fresh_made",
                  "mass_made", "mass_kept", "log_made", "logm_in", "logm_made", "logm_kept", "gap_made"))
        (keep_made, add_made, e1_made, e2_made, keep_arg, addv_made, acc_in, acc_made, acc_kept,
         e1_arg, e2_arg, add_arg, den_made, e1a_made, e2v_made, num_made, gated, den_log, den_inv, rw_made, rw_bn) = map(
            sem, ("keep_made", "add_made", "e1_made", "e2_made", "keep_arg", "addv_made", "acc_in", "acc_made", "acc_kept",
                  "e1_arg", "e2_arg", "add_arg", "den_made", "e1a_made", "e2v_made", "num_made", "gated", "den_log", "den_inv",
                  "rw_made", "rw_bn"))
        (chan_stats, head_sum, head_copied, dev_made, dev_sq, dev_sum, head_var, head_log, head_rstd,
         scale_made, shift_mul, shift_made, y_made, yhi_made, ylo_made, out_summed, x2_made) = map(
            sem, ("chan_stats", "head_sum", "head_copied", "dev_made", "dev_sq", "dev_sum", "head_var", "head_log",
                  "head_rstd", "scale_made", "shift_mul", "shift_made", "y_made", "yhi_made", "ylo_made",
                  "out_summed", "x2_made"))

        x_tiles = x.rearrange("b (n p) d -> (b n) p d", p=P)
        x2_tiles = x2.rearrange("(n p) d -> n p d", p=P)
        stage = [rw[:, :, n * D:(n + 1) * D] for n in range(4)]

        def whole(program, eng):
            program(0, True, True, False)
            with eng.Fori(1, B - 1) as b:
                program(b, True, True, True)
            program(B - 1, True, False, True)
            program(B, False, False, True)


        def groups(s, g):
            if g > 0:
                return s, g - 1
            return Step(s.b, s.i - 1, NB), C - 1

        def gated_in(s, g):
            return {0: ((Step(s.b, s.i - 1, NB), C - 1),), 1: (), 2: ((s, 0), (s, 1)), 3: ((s, 2),)}[g]

        def measured_in(s, g):
            before = Step(s.b, s.i - 1, NB)
            return {0: ((before, 2),), 1: ((before, 3),), 2: (), 3: ((s, 0), (s, 1))}[g]

        block = ctx.enter_context(nc.Block())

        @block.sync
        def _(sp):
            def load_x(s, n, ahead):
                sp.wait_ge(x_turned, known(s.nth(n - 1, TT, ahead)))
                tile = x_tiles[bass.ds(s.b * (NB * TT) + ((s.i + ahead) * TT + n), 1)]
                sp.dma_start(xin[:, n % 2:n % 2 + 1, :], tile.rearrange("o p d -> p o d")).then_inc(x_loaded[n % 2], 16)

            first = Step(0, 0, NB)
            load_x(first, 0, 0)
            load_x(first, 1, 0)
            with nc.allow_non_contiguous_dma(reason="per-channel vectors, once"):
                for n, m in enumerate(mix_in):
                    sp.dma_start(mixc[:, n, :], m.rearrange("(c p) -> p c", p=P)).then_inc(const_loaded, 16)
                for tile, src in ((decay, decay_in), (bonus, first_in), (gamma, gamma_in), (beta, beta_in)):
                    sp.dma_start(tile[:], src.rearrange("(c p) -> p c", p=P)).then_inc(const_loaded, 16)
            for n in range(4):
                sp.dma_start(stage[n], wT_in[n].rearrange("(c p) d -> p c d", p=P)).then_inc(w_loaded[n], 16)
                if n == 1:
                    load_x(first, 2, 0)
                    load_x(first, 3, 0)
            load_x(first, 0, 1)
            load_x(first, 1, 1)
            sp.sem_inc(x2_stored, 16 * FREE)

            def program(b, here, more, behind):
                for i in range(NB):
                    s = Step(b, i, NB)
                    if here and (more or i < NB - 1):
                        load_x(s, 2, 1)
                        load_x(s, 3, 1)
                    if here and (more or i < NB - 2):
                        load_x(s, 0, 2)
                        load_x(s, 1, 2)
                    if behind:
                        for n in range(TT + 2):
                            if n < TT:
                                sp.wait_ge(x2_made, known(s.nth(n - 1, TT, -NB) + FREE))
                                tile = x_tiles[bass.ds(b * (NB * TT) + ((i - NB) * TT + n), 1)]
                                sp.dma_start(xres[:, n % 2:n % 2 + 1, :],
                                             tile.rearrange("o p d -> p o d")).then_inc(xres_loaded[n % 2], 16)
                            if n >= 2:
                                sp.wait_ge(x2_made, known(s.nth(n - 1, TT, -NB) + FREE))
                                tile = x2_tiles[bass.ds(b * (NB * TT) + ((i - NB) * TT + n - 2), 1)]
                                sp.dma_start(tile.rearrange("o p d -> p o d"),
                                             xout[:]).then_inc(x2_stored, 16)

            whole(program, sp)
            sp.wait_ge(x2_stored, 16 * (B * NB * TT + FREE))

        @block.gpsimd
        def _(pool):
            g_ = nc.gpsimd
            g_.memset(ident[:], 0.0).then_inc(ident_zero, 1)
            g_.memset(same_head[:], 1.0 / HD).then_inc(ident_zero, 1)
            pool.wait_ge(ident_zero, 2)
            g_.affine_select(out=ident[:], in_=ident[:], compare_op=ALU.not_equal, fill=1.0, base=0,
                             pattern=[[-1, P]], channel_multiplier=1).then_inc(ident_made, 1)
            heads = same_head[:].rearrange("p (h k) -> p h k", k=HD)
            g_.affine_select(out=heads, in_=heads, compare_op=ALU.is_ge, fill=0.0, base=0,
                             pattern=[[-HD, P // HD], [0, HD]], channel_multiplier=1).then_inc(ident_made, 1)
            pool.wait_ge(ident_made, 2)
            g_.affine_select(out=heads, in_=heads, compare_op=ALU.is_ge, fill=0.0, base=HD - 1,
                             pattern=[[HD, P // HD], [0, HD]], channel_multiplier=-1).then_inc(ident_made, 1)

            def weight_low(n):
                for c in range(C):
                    pool.wait_ge(w_hi_made, C * n + c + 1)
                    g_.tensor_tensor(w_lo[:, n, c, :], stage[n][:, c, :], w_hi[:, n, c, :].bitcast(F32),
                                     ALU.subtract).then_inc(w_lo_kr, 1)

            def mix_low(s, kind, ahead, c):
                pool.wait_ge(hi_made, known(s.nth(C * kind + c + 1, 3 * C, ahead)))
                g_.tensor_tensor(mix_lo[:, c, :], mixed[:, c % MIX, :], mix_hi[:, c, :].bitcast(F32),
                                 ALU.subtract).then_inc(lo_made, 1)

            def fresh_argument(s, g):
                pool.wait_ge(peak_made, known(s.nth(g + 1, C)))
                pool.wait_ge(acc_made, known(s.nth(g - 1, C)))
                g_.tensor_tensor(E[:, g % 2, :], kk[:, g, :], M[:, g % 2, 1:], ALU.subtract).then_inc(fresh_arg, 1)

            def log_mass(s, g):
                pool.wait_ge(log_made, known(s.nth(g + 1, C)))
                g_.tensor_tensor(S_[:, g % 2, 1:], M[:, g % 2, 1:], S_[:, g % 2, 1:], ALU.add).then_inc(logm_made, 1)

            def weigh(s, g):
                pool.wait_ge(den_made, known(s.nth(g + 1, C)))
                pool.wait_ge(acc_kept, known(s.nth(g + 1, C)))
                g_.tensor_tensor(S_[:, g % 2, 1:], S_[:, g % 2, 1:], acc[:, g % 2, 0:T], ALU.mult).then_inc(e1a_made, 1)
                g_.tensor_tensor(M[:, g % 2, 0:T], M[:, g % 2, 0:T], vv[:, g, :], ALU.mult).then_inc(e2v_made, 1)

            def gate(s, g):
                rows = slice(s.i % NB * T, (s.i % NB + 1) * T)
                pool.wait_ge(kind_out, known(s.nth(C * KIND_R + g + 1, 3 * C)))
                pool.wait_ge(rw_made, known(s.nth(g + 1, C)))
                g_.tensor_tensor(rw[:, g, rows], rw[:, g, rows], sig[:, g, :], ALU.mult).then_inc(gated, 1)

            def y_low(s, n):
                pool.wait_ge(yhi_made, known(s.nth(n + 1, TT, -NB)))
                g_.tensor_tensor(y_lo[:, n % 2], y[:, :, n * P:(n + 1) * P], y_hi[:, n % 2].bitcast(F32),
                                 ALU.subtract).then_inc(ylo_made, 1)

            def program(b, here, more, behind):
                for i in range(NB):
                    s = Step(b, i, NB)
                    ahead = here and (more or i < NB - 1)
                    for g in range(C):
                        sb_, gb = groups(s, g)
                        before = behind if i == 0 else here
                        back = here if g > 0 else before
                        kind, by = {0: (KIND_R, 0), 1: (None, 0), 2: (KIND_K, 1), 3: (KIND_V, 1)}[g]
                        mixing = kind is not None and (ahead if by else here)
                        gates_now = [pn for pn in gated_in(s, g) if (here if pn[0] is s else before)]
                        if here:
                            fresh_argument(s, g)
                        if behind and i > 0 and g == 3:
                            y_low(s, 2)
                            y_low(s, 3)
                        if mixing and g != 2:
                            mix_low(s, kind, by, 0)
                        for p, n in gates_now[:-1]:
                            gate(p, n)
                        if back:
                            weigh(sb_, gb)
                        if here:
                            log_mass(s, g)
                        if mixing:
                            if g == 2:
                                mix_low(s, kind, by, 0)
                            mix_low(s, kind, by, 1)
                        if behind and i > 0 and g == 1:
                            y_low(s, 0)
                            y_low(s, 1)
                        for p, n in gates_now[-1:]:
                            gate(p, n)
                        if mixing:
                            mix_low(s, kind, by, 2)
                            mix_low(s, kind, by, 3)
                        if behind and i == 0 and g >= 2:
                            y_low(s, 2 * g - 4)
                            y_low(s, 2 * g - 3)

            first = Step(0, 0, NB)
            weight_low(KIND_K)
            for kind in (KIND_K, KIND_V):
                for c in range(C):
                    mix_low(first, kind, 0, c)
            weight_low(KIND_R)
            whole(program, pool)

        @block.tensor
        def _(pe):
            def turn(s, n, ahead=0):
                pe.wait_ge(xnormed, known(s.nth(n + 1, TT, ahead)))
                pe.wait_ge(xT_made, known(s.nth(n - 1, TT, ahead)))
                for c in range(C):
                    mm = pe.transpose(tp_ps[n % 2][:, c, :], xin[:, n % 2, c * P:(c + 1) * P], ident[:])
                mm.then_inc(x_turned, 1)

            def project(s, kind, ahead=0):
                for c in range(C):
                    pe.wait_ge(lo_made, known(s.nth(C * kind + c + 1, 3 * C, ahead)))
                    for g in range(C):
                        if c == 0:
                            pe.wait_ge(kind_out, known(s.nth(C * kind + g + 1 - C, 3 * C, ahead)))
                        cols = slice(g * P, (g + 1) * P)
                        hi, lo = w_hi[:, kind, c, cols], w_lo[:, kind, c, cols]
                        pe.matmul(acc_ps[g][:], hi, mix_hi[:, c, :], start=(c == 0), stop=False)
                        pe.matmul(acc_ps[g][:], hi, mix_lo[:, c, :], start=False, stop=False)
                        mm = pe.matmul(acc_ps[g][:], lo, mix_hi[:, c, :], start=False, stop=(c == C - 1))
                        if c == C - 1:
                            mm.then_inc(kind_summed, 1)
                    if c < C - 1:
                        mm.then_inc(chunk_used, 1)

            def head_sums(b):
                pe.wait_ge(chan_stats, b * 1)
                pe.wait_ge(x2_made, known(Step(b, 0, NB).nth(-1, TT, -NB) + FREE))
                pe.matmul(out_ps[0][:, 0:2 * C], same_head[:], mv_rw[:].rearrange("p a c -> p (a c)"),
                          start=True, stop=True).then_inc(head_sum, 1)
                pe.wait_ge(dev_sq, b * 1)
                pe.matmul(out_ps[0][:, 2 * C:3 * C], same_head[:], dev2[:], start=True, stop=True).then_inc(dev_sum, 1)

            def out_product(s, n):
                if n == 0:
                    pe.wait_ge(head_var, s.b * 1)
                pe.wait_ge(ylo_made, known(s.nth(n + 1, TT, -NB)))
                pe.wait_ge(x2_made, known(s.nth(n - 1, TT, -NB) + FREE))
                for g in range(C):
                    hi, lo = y_hi[:, n % 2, g, :], y_lo[:, n % 2, g, :]
                    pe.matmul(out_ps[n % 2][:], hi, w_hi[:, 3, g, :], start=(g == 0), stop=False)
                    pe.matmul(out_ps[n % 2][:], hi, w_lo[:, 3, g, :], start=False, stop=False)
                    mm = pe.matmul(out_ps[n % 2][:], lo, w_hi[:, 3, g, :], start=False, stop=(g == C - 1))
                mm.then_inc(out_summed, 1)

            def program(b, here, more, behind):
                for i in range(NB):
                    s = Step(b, i, NB)
                    ahead = here and (more or i < NB - 1)
                    if ahead:
                        turn(s, 0, 1)
                        turn(s, 1, 1)
                    if here:
                        project(s, KIND_R)
                    if behind and i == 0:
                        head_sums(b)
                    if ahead:
                        turn(s, 2, 1)
                        turn(s, 3, 1)
                    if behind and i > 0:
                        out_product(s, 0)
                        out_product(s, 1)
                    if ahead:
                        project(s, KIND_K, 1)
                    if behind and i == 0:
                        out_product(s, 0)
                        out_product(s, 1)
                    if behind and i > 0:
                        out_product(s, 2)
                        out_product(s, 3)
                    if ahead:
                        project(s, KIND_V, 1)
                    if behind and i == 0:
                        out_product(s, 2)
                        out_product(s, 3)

            first = Step(0, 0, NB)
            pe.sem_inc(out_summed, FREE)
            pe.wait_ge(ident_made, 3)
            for n in range(TT):
                turn(first, n)
            pe.wait_ge(w_lo_kr, C)
            project(first, KIND_K)
            pe.wait_ge(w_lo_vo, C)
            project(first, KIND_V)
            pe.wait_ge(w_lo_kr, 2 * C)
            pe.wait_ge(w_lo_vo, 2 * C)
            whole(program, pe)

        @block.scalar
        def _(act):
            f = nc.scalar.activation
            act.preload_act_table_set(LOG_EXP)

            def copy_turned(s, n, ahead=0):
                act.wait_ge(x_turned, known(s.nth(n + 1, TT, ahead)))
                if n == 0:
                    act.wait_ge(shift_kept, known(s.nth(1, 1, ahead)))
                f(xT[:, :, 1 + n * P:1 + (n + 1) * P], tp_ps[n % 2][:], ACT.Copy).then_inc(xT_made, 1)

            def x_rstd(s, pair, ahead=0):
                act.wait_ge(xstat, known(s.nth(pair + 1, 2, ahead)))
                f(ln_x[:], mv_x[:, :, 1], ACT.Ln, bias=ln_eps[:]).then_inc(xlog, 1)
                act.wait_ge(xlog, known(s.nth(pair + 1, 2, ahead)))
                f(rstd_x[:], ln_x[:], ACT.Exp, scale=-0.5).then_inc(xrstd, 1)

            def mix_high(s, kind, ahead, c):
                act.wait_ge(mix_made, known(s.nth(C * kind + c + 1, 3 * C, ahead)))
                if c < C - 1:
                    act.wait_ge(chunk_used, known(s.nth((C - 1) * (kind - 1) + c + 1, 3 * (C - 1), ahead)))
                else:
                    act.wait_ge(kind_summed, known(s.nth(C * kind, 3 * C, ahead)))
                f(mix_hi[:, c, :], mixed[:, c % MIX, :], ACT.Copy).then_inc(hi_made, 1)

            def copy_k(s, g, ahead=0):
                act.wait_ge(kind_summed, known(s.nth(C * KIND_K + g + 1, 3 * C, ahead)))
                act.wait_ge(gap_made, known(s.nth(g + 1, C, ahead - 1)))
                f(kk[:, g, :], acc_ps[g][:], ACT.Copy).then_inc(kind_out, 1)

            def copy_v(s, g, ahead=0):
                act.wait_ge(kind_summed, known(s.nth(C * KIND_V + g + 1, 3 * C, ahead)))
                act.wait_ge(e2v_made, known(s.nth(g + 1, C, ahead - 1)))
                f(vv[:, g, :], acc_ps[g][:], ACT.Copy).then_inc(kind_out, 1)

            def copy_r(s, g):
                act.wait_ge(kind_summed, known(s.nth(C * KIND_R + g + 1, 3 * C)))
                act.wait_ge(gated, known(s.nth(g + 1, C, -1)))
                f(sig[:, g, :], acc_ps[g][:], ACT.Sigmoid).then_inc(kind_out, 1)

            def fade(s, g):
                act.wait_ge(fade_arg, known(s.nth(g + 1, C)))
                f(A[:, g % 2, :], A[:, g % 2, :], ACT.Exp).then_inc(fade_made, 1)

            def fresh(s, g):
                act.wait_ge(fresh_arg, known(s.nth(g + 1, C)))
                f(E[:, g % 2, :], E[:, g % 2, :], ACT.Exp).then_inc(fresh_made, 1)

            def mass_log(s, g):
                act.wait_ge(mass_kept, known(s.nth(g + 1, C)))
                f(S_[:, g % 2, 1:], S_[:, g % 2, 1:], ACT.Ln, bias=eps[:]).then_inc(log_made, 1)

            def gates(s, g):
                j, n = g % 2, known(s.nth(g + 1, C))
                act.wait_ge(logm_kept, n)
                f(S_[:, j, 1:], M[:, j, 0:T], ACT.Relu, bias=bonus[:, g:g + 1], scale=-1.0).then_inc(e1_arg, 1)
                act.wait_ge(keep_arg, n)
                f(A[:, j, :], A[:, j, :], ACT.Exp).then_inc(keep_made, 1)
                act.wait_ge(add_arg, n)
                f(E[:, j, :], E[:, j, :], ACT.Exp, scale=-1.0).then_inc(add_made, 1)
                act.wait_ge(e1_arg, n)
                f(M[:, j, 0:T], M[:, j, 0:T], ACT.Relu, bias=neg_bonus[:, g:g + 1]).then_inc(e2_arg, 1)
                f(S_[:, j, 1:], S_[:, j, 1:], ACT.Exp, scale=-1.0).then_inc(e1_made, 1)
                act.wait_ge(e2_arg, n)
                f(M[:, j, 0:T], M[:, j, 0:T], ACT.Exp, scale=-1.0).then_inc(e2_made, 1)

            def inverse(s, g):
                act.wait_ge(den_made, known(s.nth(g + 1, C)))
                f(A[:, g % 2, :], A[:, g % 2, :], ACT.Ln).then_inc(den_log, 1)
                act.wait_ge(den_log, known(s.nth(g + 1, C)))
                f(A[:, g % 2, :], A[:, g % 2, :], ACT.Exp, scale=-1.0).then_inc(den_inv, 1)

            def head_rstds(b):
                act.wait_ge(head_var, b * 1)
                f(ln_h[:], var_h[:], ACT.Ln, bias=ln_eps[:]).then_inc(head_log, 1)
                act.wait_ge(head_log, b * 1)
                f(rstd_h[:], ln_h[:], ACT.Exp, scale=-0.5).then_inc(head_rstd, 1)

            def y_high(s, n):
                act.wait_ge(y_made, known(s.nth(C, C, -NB)))
                act.wait_ge(out_summed, known(s.nth(n - 1, TT, -NB) + FREE))
                f(y_hi[:, n % 2], y[:, :, n * P:(n + 1) * P], ACT.Copy).then_inc(yhi_made, 1)

            def program(b, here, more, behind):
                for i in range(NB):
                    s = Step(b, i, NB)
                    ahead = here and (more or i < NB - 1)
                    for g in range(C):
                        sb_, gb = groups(s, g)
                        before = behind if i == 0 else here
                        back = here if g > 0 else before
                        kind, by = {0: (KIND_R, 0), 1: (None, 0), 2: (KIND_K, 1), 3: (KIND_V, 1)}[g]
                        mixing = kind is not None and (ahead if by else here)
                        if here:
                            fade(s, g)
                            fresh(s, g)
                        if mixing and g != 2:
                            mix_high(s, kind, by, 0)
                        if back:
                            inverse(sb_, gb)
                        if here:
                            mass_log(s, g)
                        if ahead and g < 2:
                            x_rstd(s, g, 1)
                        if behind and g == 1 and i == 0:
                            head_rstds(b)
                        if behind and (i, g) == (0, 2) or behind and i > 0 and g == 0:
                            y_high(s, 0)
                            y_high(s, 1)
                        if mixing:
                            if g == 2:
                                mix_high(s, kind, by, 0)
                            mix_high(s, kind, by, 1)
                            mix_high(s, kind, by, 2)
                        if here:
                            gates(s, g)
                        if behind and (i, g) == (0, 3) or behind and i > 0 and g == 2:
                            y_high(s, 2)
                            y_high(s, 3)
                        if mixing:
                            mix_high(s, kind, by, 3)
                        if ahead and g < 2:
                            copy_turned(s, 2 * g, 1)
                            copy_turned(s, 2 * g + 1, 1)
                        if here and g == 0:
                            for n in range(C):
                                copy_v(s, n)
                        if here and g == 1:
                            for n in range(C):
                                copy_r(s, n)
                            act.preload_act_table_set(LOG_EXP)
                        if ahead and g == 3:
                            for n in range(C):
                                copy_k(s, n, 1)

            def weight_high(n):
                act.wait_ge(w_loaded[n], 16)
                for c in range(C):
                    f(w_hi[:, n, c, :], stage[n][:, c, :], ACT.Copy).then_inc(w_hi_made, 1)

            first = Step(0, 0, NB)
            act.wait_ge(const_made, 2)
            x_rstd(first, 0)
            act.wait_ge(const_loaded, 16 * 7)
            f(neg_decay[:], decay[:], ACT.Exp).then_inc(decay_exp, 1)
            copy_turned(first, 0)
            copy_turned(first, 1)
            weight_high(KIND_K)
            x_rstd(first, 1)
            copy_turned(first, 2)
            copy_turned(first, 3)
            weight_high(KIND_V)
            for c in range(C):
                mix_high(first, KIND_K, 0, c)
            weight_high(KIND_R)
            for g in range(C):
                copy_k(first, g)
            for c in range(C):
                mix_high(first, KIND_V, 0, c)
            weight_high(3)
            whole(program, act)

        @block.vector
        def _(dve):
            v = nc.vector
            v.memset(eps[:], EPS).then_inc(const_made, 1)
            v.memset(ln_eps[:], LN_EPS).then_inc(const_made, 1)
            dve.sem_inc(x2_made, FREE)

            def x_stats(s, pair, ahead=0):
                for n in (2 * pair, 2 * pair + 1):
                    dve.wait_ge(x_loaded[n % 2], known(s.nth(n // 2 + 1, TT // 2, ahead) * 16))
                    v.bn_stats(bn_x[:, n % 2, :], xin[:, n % 2, :]).then_inc(xbn, 1)
                for n in (2 * pair, 2 * pair + 1):
                    dve.wait_ge(xbn, known(s.nth(n + 1, TT, ahead)))
                    dve.sem_inc(passed, 1)
                    ins = v.bn_aggr(mv_x[:, n % 2, :], bn_x[:, n % 2, :])
                ins.then_inc(xstat, 1)

            def x_norm(s, pair, ahead=0):
                dve.wait_ge(xrstd, known(s.nth(pair + 1, 2, ahead)))
                for n in (2 * pair, 2 * pair + 1):
                    v.tensor_scalar(xin[:, n % 2, :], xin[:, n % 2, :], mv_x[:, n % 2, 0:1], rstd_x[:, n % 2:n % 2 + 1],
                                    ALU.subtract, ALU.mult).then_inc(xnormed, 1)

            def keep_shift(s, ahead=0):
                dve.wait_ge(mix_made, known(s.nth(0, 3 * C, ahead)))
                if (s.i + ahead) % NB == 0:
                    v.memset(xT[:, :, 0:1], 0.0).then_inc(shift_kept, 1)
                else:
                    v.tensor_copy(xT[:, :, 0:1], xT[:, :, T:T + 1]).then_inc(shift_kept, 1)

            def difference(s, ahead=0):
                dve.wait_ge(xT_made, known(s.nth(TT, TT, ahead)))
                for c in range(C):
                    v.tensor_tensor(xd[:, c, :], xT[:, c, 1:], xT[:, c, 0:T], ALU.subtract).then_inc(diff_made, 1)

            def mix(s, kind, ahead, c):
                dve.wait_ge(diff_made, known(s.nth(c + 1, C, ahead)))
                if c % MIX == 0:
                    dve.wait_ge(lo_made, known(s.nth(C * kind + c // MIX, 3 * C, ahead)))
                v.scalar_tensor_tensor(mixed[:, c % MIX, :], xd[:, c, :], mixc[:, kind, c:c + 1], xT[:, c, 0:T],
                                       ALU.mult, ALU.add).then_inc(mix_made, 1)

            def start_front():
                for tile, value in ((peak_c, LOWEST), (logm_c, LOWEST), (mass_c, 1.0)):
                    ins = v.memset(tile[:], value)
                ins.then_inc(start_set, 1)

            def peak(s, g):
                j = g % 2
                if s.i == 0 and g == 0:
                    dve.wait_ge(logm_kept, known(s.nth(0, C)))
                    start_front()
                    dve.wait_ge(start_set, s.b + 1)
                dve.wait_ge(num_made, known(s.nth(g - 1, C)))
                v.tensor_copy(M[:, j, 0:1], peak_c[:, g:g + 1]).then_inc(peak_in, 1)
                dve.wait_ge(kind_out, known(s.nth(C * KIND_K + g + 1, 3 * C)))
                v.tensor_tensor_scan(M[:, j, 1:], decay[:, g:g + 1].to_broadcast([P, T]), kk[:, g, :],
                                     peak_c[:, g:g + 1], ALU.add, ALU.max).then_inc(peak_made, 1)

            def fade(s, g):
                j = g % 2
                dve.wait_ge(peak_made, known(s.nth(g + 1, C)))
                dve.wait_ge(rw_made, known(s.nth(g - 1, C)))
                v.scalar_tensor_tensor(A[:, j, :], M[:, j, 0:T], decay[:, g:g + 1], M[:, j, 1:],
                                       ALU.add, ALU.subtract).then_inc(fade_arg, 1)
                v.tensor_copy(peak_c[:, g:g + 1], M[:, j, T:T + 1]).then_inc(peak_kept, 1)

            def mass(s, g):
                j = g % 2
                dve.wait_ge(fresh_made, known(s.nth(g + 1, C)))
                v.tensor_tensor_scan(S_[:, j, 1:], A[:, j, :], E[:, j, :], mass_c[:, g:g + 1],
                                     ALU.mult, ALU.add).then_inc(mass_made, 1)
                v.tensor_copy(S_[:, j, 0:1], logm_c[:, g:g + 1]).then_inc(logm_in, 1)
                dve.wait_ge(mass_made, known(s.nth(g + 1, C)))
                v.tensor_copy(mass_c[:, g:g + 1], S_[:, j, T:T + 1]).then_inc(mass_kept, 1)

            def gap(s, g):
                j = g % 2
                dve.wait_ge(logm_made, known(s.nth(g + 1, C)))
                dve.wait_ge(peak_kept, known(s.nth(g + 1, C)))
                v.tensor_tensor(M[:, j, 0:T], S_[:, j, 0:T], kk[:, g, :], ALU.subtract).then_inc(gap_made, 1)
                v.tensor_copy(logm_c[:, g:g + 1], S_[:, j, T:T + 1]).then_inc(logm_kept, 1)
                dve.wait_ge(gap_made, known(s.nth(g + 1, C)))
                v.tensor_scalar(A[:, j, :], M[:, j, 0:T], decay[:, g:g + 1], 0.0, ALU.add, ALU.min).then_inc(keep_arg, 1)
                v.tensor_scalar(E[:, j, :], M[:, j, 0:T], decay[:, g:g + 1], 0.0, ALU.add, ALU.max).then_inc(add_arg, 1)

            def add_v(s, g):
                j = g % 2
                dve.wait_ge(kind_out, known(s.nth(C * KIND_V + g + 1, 3 * C)))
                dve.wait_ge(add_made, known(s.nth(g + 1, C)))
                v.tensor_tensor(E[:, j, :], E[:, j, :], vv[:, g, :], ALU.mult).then_inc(addv_made, 1)

            def accumulate(s, g):
                j = g % 2
                dve.wait_ge(e1a_made, known(s.nth(g - 1, C)))
                v.tensor_copy(acc[:, j, 0:1], acc_c[:, g:g + 1]).then_inc(acc_in, 1)
                dve.wait_ge(addv_made, known(s.nth(g + 1, C)))
                v.tensor_tensor_scan(acc[:, j, 1:], A[:, j, :], E[:, j, :], acc_c[:, g:g + 1],
                                     ALU.mult, ALU.add).then_inc(acc_made, 1)

            def denominator(s, g):
                j = g % 2
                dve.wait_ge(e2_made, known(s.nth(g + 1, C)))
                dve.wait_ge(acc_made, known(s.nth(g + 1, C)))
                v.scalar_tensor_tensor(A[:, j, :], M[:, j, 0:T], EPS, S_[:, j, 1:],
                                       ALU.add, ALU.add).then_inc(den_made, 1)
                v.tensor_copy(acc_c[:, g:g + 1], acc[:, j, T:T + 1]).then_inc(acc_kept, 1)

            def numerator(s, g):
                j = g % 2
                dve.wait_ge(e2v_made, known(s.nth(g + 1, C)))
                v.tensor_tensor(S_[:, j, 1:], S_[:, j, 1:], M[:, j, 0:T], ALU.add).then_inc(num_made, 1)

            def result(s, g):
                j, rows = g % 2, slice(s.i % NB * T, (s.i % NB + 1) * T)
                dve.wait_ge(den_inv, known(s.nth(g + 1, C)))
                dve.wait_ge(num_made, known(s.nth(g + 1, C)))
                dve.wait_ge(y_made, known(s.nth(g + 1, C, -NB)))
                v.tensor_tensor(rw[:, g, rows], S_[:, j, 1:], A[:, j, :], ALU.mult).then_inc(rw_made, 1)

            def measure(s, g):
                rows = slice(s.i % NB * T, (s.i % NB + 1) * T)
                dve.wait_ge(gated, known(s.nth(g + 1, C)))
                v.bn_stats(bn_rw[:, g, s.i % NB, :], rw[:, g, rows]).then_inc(rw_bn, 1)

            def channel_stats(b):
                dve.wait_ge(rw_bn, b * (NB * C))
                dve.sem_inc(passed, 1)
                for g in range(C):
                    ins = v.bn_aggr(mv_rw[:, :, g], bn_rw[:, g].rearrange("p n k -> p (n k)"))
                ins.then_inc(chan_stats, 1)

            def head_deviation(b):
                dve.wait_ge(head_sum, b * 1)
                v.tensor_copy(mv_head[:].rearrange("p a c -> p (a c)"), out_ps[0][:, 0:2 * C]).then_inc(head_copied, 1)
                dve.wait_ge(head_copied, b * 1)
                v.tensor_tensor(dev[:], mv_rw[:, 0, :], mv_head[:, 0, :], ALU.subtract).then_inc(dev_made, 1)
                dve.wait_ge(dev_made, b * 1)
                v.tensor_tensor(dev2[:], dev[:], dev[:], ALU.mult).then_inc(dev_sq, 1)

            def head_variance(b):
                dve.wait_ge(dev_sum, b * 1)
                v.tensor_tensor(var_h[:], out_ps[0][:, 2 * C:3 * C], mv_head[:, 1, :], ALU.add).then_inc(head_var, 1)

            def head_affine(b):
                dve.wait_ge(head_rstd, b * 1)
                v.tensor_tensor(scale_h[:], rstd_h[:], gamma[:], ALU.mult).then_inc(scale_made, 1)
                dve.wait_ge(scale_made, b * 1)
                v.tensor_tensor(mean_s[:], mv_head[:, 0, :], scale_h[:], ALU.mult).then_inc(shift_mul, 1)
                dve.wait_ge(shift_mul, b * 1)
                v.tensor_tensor(shift_h[:], beta[:], mean_s[:], ALU.subtract).then_inc(shift_made, 1)
                dve.wait_ge(shift_made, b * 1)

            def normed(s):
                dve.wait_ge(ylo_made, known(s.nth(TT, TT, -NB - 1)))
                for g in range(C):
                    v.tensor_scalar(y[:, g, :], rw[:, g, s.i * T:(s.i + 1) * T], scale_h[:, g:g + 1], shift_h[:, g:g + 1],
                                    ALU.mult, ALU.add).then_inc(y_made, 1)

            def residual(s, n):
                dve.wait_ge(xres_loaded[n % 2], known(s.nth(n // 2 + 1, TT // 2, -NB) * 16))
                dve.wait_ge(x2_stored, known((s.nth(n, TT, -NB) + FREE) * 16))
                dve.wait_ge(out_summed, known(s.nth(n + 1, TT, -NB) + FREE))
                v.tensor_tensor(xout[:, 0, :], out_ps[n % 2][:], xres[:, n % 2, :], ALU.add).then_inc(x2_made, 1)

            def program(b, here, more, behind):
                for i in range(NB):
                    s = Step(b, i, NB)
                    ahead = here and (more or i < NB - 1)
                    for g in range(C):
                        sb_, gb = groups(s, g)
                        before = behind if i == 0 else here
                        back = here if g > 0 else before
                        kind, by = {0: (KIND_R, 0), 1: (None, 0), 2: (KIND_K, 1), 3: (KIND_V, 1)}[g]
                        mixing = kind is not None and (ahead if by else here)
                        if here:
                            peak(s, g)
                        if back:
                            add_v(sb_, gb)
                        if here:
                            fade(s, g)
                        for p, n in measured_in(s, g):
                            if (here if p is s else before):
                                measure(p, n)
                        if behind and g == 1 and i == 0:
                            channel_stats(b)
                        if back:
                            accumulate(sb_, gb)
                        if mixing and g != 2:
                            mix(s, kind, by, 0)
                        if back:
                            denominator(sb_, gb)
                        if ahead and g < 2:
                            x_stats(s, g, 1)
                        if here:
                            mass(s, g)
                        if behind and g == 1 and i == 0:
                            head_deviation(b)
                        if behind and g == 0 and i > 0:
                            normed(s)
                        if ahead and g == 2:
                            difference(s, 1)
                            mix(s, kind, by, 0)
                        if mixing:
                            mix(s, kind, by, 1)
                            mix(s, kind, by, 2)
                        if ahead and g < 2:
                            x_norm(s, g, 1)
                        if behind and i > 0 and g >= 2:
                            residual(s, 2 * g - 4)
                        if behind and (i, g) == (0, 3):
                            residual(s, 0)
                        if behind and (i, g) == (1, 0):
                            residual(Step(b, 0, NB), 2)
                        if back:
                            numerator(sb_, gb)
                        if behind and g == 1 and i == 0:
                            head_variance(b)
                        if here:
                            gap(s, g)
                        if behind and g == 1 and i == 0:
                            head_affine(b)
                            normed(s)
                        if mixing:
                            mix(s, kind, by, 3)
                        if ahead and g == 0:
                            keep_shift(s, 1)
                        if back:
                            result(sb_, gb)
                        if behind and i > 0 and g >= 2:
                            residual(s, 2 * g - 3)
                        if behind and (i, g) == (0, 3):
                            residual(s, 1)
                        if behind and (i, g) == (1, 0):
                            residual(Step(b, 0, NB), 3)
                        if i == 0 and g == 0:
                            v.memset(acc_c[:], 0.0).then_inc(acc_start, 1)
                            dve.wait_ge(acc_start, b + 1)

            def weight_low(n):
                for c in range(C):
                    dve.wait_ge(w_hi_made, C * n + c + 1)
                    v.tensor_tensor(w_lo[:, n, c, :], stage[n][:, c, :], w_hi[:, n, c, :].bitcast(F32),
                                    ALU.subtract).then_inc(w_lo_vo, 1)

            first = Step(0, 0, NB)
            keep_shift(first)
            x_stats(first, 0)
            x_norm(first, 0)
            dve.wait_ge(decay_exp, 1)
            v.tensor_scalar(decay[:], neg_decay[:], -1.0, None, ALU.mult)
            v.tensor_scalar(neg_bonus[:], bonus[:], -1.0, None, ALU.mult).then_inc(bonus_neg, 1)
            dve.wait_ge(bonus_neg, 1)
            x_stats(first, 1)
            x_norm(first, 1)
            difference(first)
            for c in range(C):
                mix(first, KIND_K, 0, c)
            weight_low(KIND_V)
            for c in range(C):
                mix(first, KIND_V, 0, c)
            weight_low(3)
            dve.wait_ge(w_lo_kr, 2 * C)
            whole(program, dve)


def feed_forward(nc, sem, x2, w1, w3, w2, out, B, S):
    E, D, F = w1.shape
    C = D // P
    FC = F // P
    CAP = S // E
    N = B * CAP
    NT = N // P
    TB = CAP // P
    NH = N // T
    R = 3
    LN_AT = (0, 1, 3, 4)

    with ExitStack() as ctx:
        def sb(name, shape, dt=F32):
            return ctx.enter_context(nc.sbuf_tensor(name, shape, dt))

        def psum(name, shape):
            return ctx.enter_context(nc.psum_tensor(name, shape, F32))

        ident = sb("ident2", [P, P])
        ln_eps = sb("ln_eps2", [P, 1])
        w13_in = sb("w13_in", [P, 2, 2, C, P])
        w13_hi = sb("w13_hi", [P, R, 2, C, P], F32R)
        w13_lo = sb("w13_lo", [P, R, 2, C, P], F32R)
        w2_in = sb("w2_in", [P, 2, D])
        w2_hi = sb("w2_hi", [P, FC, D], F32R)
        w2_lo = sb("w2_lo", [P, FC, D], F32R)
        xt = sb("xt", [P, 2, TB, D])
        bn = sb("bn", [P, TB, 6])
        mv = sb("mv", [P, TB, 2])
        lnv = sb("lnv", [P, TB])
        rstd = sb("rstd", [P, TB])
        xT_hi = sb("xT_hi", [P, C, N], F32R)
        xT_lo = sb("xT_lo", [P, C, N], F32R)
        gated = sb("gated2", [P, 2, T])
        hid = sb("hid", [P, FC, N])
        hid_hi = sb("hid_hi", [P, 2, FC, P], F32R)
        hid_lo = sb("hid_lo", [P, 2, FC, P], F32R)
        xres = sb("xres2", [P, 2, D])
        xout = sb("xout2", [P, 2, D])

        gate_ps = [psum(f"gate_ps{n}", [P, T]) for n in range(2)]
        up_ps = [psum(f"up_ps{n}", [P, T]) for n in range(2)]
        turn_ps = [psum(f"turn_ps{n}", [P, C, P]) for n in range(2)]
        down_ps = [psum(f"down_ps{n}", [P, D]) for n in range(2)]

        passed = sem("passed2")
        w13_loaded, w2_loaded, xt_loaded, res_loaded, out_stored = (
            [sem(f"{name}{n}") for n in range(2)]
            for name in ("w13_loaded", "w2_loaded", "xt_loaded", "res_loaded", "out_stored"))
        (id_zero, id_made, eps_made, w13_high, w13_low, w2_high, w2_low) = map(
            sem, ("id_zero", "id_made", "eps_made", "w13_high", "w13_low", "w2_high", "w2_low"))
        (bn_done, stat_done, log_done, rstd_done, norm_done, turned, xT_high, xT_low) = map(
            sem, ("bn_done", "stat_done", "log_done", "rstd_done", "norm_done", "turned", "xT_high", "xT_low"))
        (gate_summed, up_summed, silu_made, hid_made, hid_high, hid_low, down_summed, out_made) = map(
            sem, ("gate_summed", "up_summed", "silu_made", "hid_made", "hid_high", "hid_low", "down_summed", "out_made"))

        def whole(program, eng):
            with eng.Fori(0, E - 1) as e:
                program(e, True)
            program(E - 1, False)

        def ring(f, slots):
            f %= FC
            if f >= slots:
                return f - slots
            return max(n for n in range(FC) if n % slots == f % slots) - FC

        def nth_load(e, f):
            return e * len(range(f % 2, FC, 2)) + (f // 2 + 1)

        def tokens(t, e, n, count=1):
            m, h = divmod(n, TB)
            tiles = t.rearrange("(n p) d -> n p d", p=P)
            return tiles[bass.ds(e * TB + (m * (S // P) + h), count)].rearrange("n p d -> p n d")

        block = ctx.enter_context(nc.Block())

        @block.sync
        def _(sp):
            for stored in out_stored:
                sp.sem_inc(stored, 16 * FREE)

            def load_w13(e, f):
                prev = ring(f, 2)
                e, f = e + f // FC, f % FC
                sp.wait_ge(w13_low, known((e * FC + (prev + 1)) * 2))
                for n, w in enumerate((w1, w3)):
                    src = w.rearrange("e (c p) f -> e p c f", p=P)[bass.ds(e, 1), :, :, f * P:(f + 1) * P]
                    sp.dma_start(w13_in[:, f % 2, n], src.rearrange("o p c f -> (o p) c f")).then_inc(w13_loaded[f % 2], 16)

            def load_w2(e, f):
                prev = ring(f, 2)
                e, f = e + f // FC, f % FC
                sp.wait_ge(w2_low, known(e * FC + (prev + 1)))
                src = w2[bass.ds(e, 1), f * P:(f + 1) * P, :]
                sp.dma_start(w2_in[:, f % 2], src.rearrange("o p d -> (o p) d")).then_inc(w2_loaded[f % 2], 16)

            def load_xt(e, m):
                sp.wait_ge(turned, known(e * NT + (m - 1) * TB))
                sp.dma_start(xt[:, m % 2], tokens(x2, e, m * TB, TB)).then_inc(xt_loaded[m % 2], 16)

            load_xt(0, 0)
            load_xt(0, 1)
            load_w13(0, 0)
            load_w13(0, 1)
            load_xt(0, 2)
            load_xt(0, 3)
            load_w2(0, 0)
            load_w2(0, 1)
            load_w13(0, 2)

            def program(e, more):
                for f in range(FC):
                    if more and f in (4, 5):
                        load_xt(e + 1, f - 4)
                    if more or f + 3 < FC:
                        load_w13(e, f + 3)
                    if more or f + 2 < FC:
                        load_w2(e, f + 2)
                for n in range(NT + 2):
                    if n < NT:
                        sp.wait_ge(out_made, known(e * NT + (n - 1 + FREE)))
                        sp.dma_start(xres[:, n % 2:n % 2 + 1], tokens(x2, e, n)).then_inc(res_loaded[n % 2], 16)
                    if 2 <= n < B and more:
                        load_xt(e + 1, n)
                    if n >= 2:
                        sp.wait_ge(out_made, known(e * NT + (n - 1 + FREE)))
                        sp.dma_start(tokens(out, e, n - 2), xout[:, n % 2:n % 2 + 1]).then_inc(out_stored[n % 2], 16)

            whole(program, sp)
            for stored in out_stored:
                sp.wait_ge(stored, 16 * (E * NT // 2 + FREE))

        @block.gpsimd
        def _(pool):
            g_ = nc.gpsimd
            g_.memset(ident[:], 0.0).then_inc(id_zero, 1)
            pool.wait_ge(id_zero, 1)
            g_.affine_select(out=ident[:], in_=ident[:], compare_op=ALU.not_equal, fill=1.0, base=0,
                             pattern=[[-1, P]], channel_multiplier=1).then_inc(id_made, 1)

            def low_w13(e, f):
                e, f = e + f // FC, f % FC
                pool.wait_ge(w13_high, known((e * FC + f + 1) * 2))
                for n in range(2):
                    g_.tensor_tensor(w13_lo[:, f % R, n], w13_in[:, f % 2, n], w13_hi[:, f % R, n].bitcast(F32),
                                     ALU.subtract).then_inc(w13_low, 1)

            def low_w2(e, f):
                pool.wait_ge(w2_high, known(e * FC + (f + 1)))
                g_.tensor_tensor(w2_lo[:, f], w2_in[:, f % 2], w2_hi[:, f].bitcast(F32), ALU.subtract).then_inc(w2_low, 1)

            low_w13(0, 0)
            low_w13(0, 1)

            def program(e, more):
                for f in range(FC):
                    if more or f + 2 < FC:
                        low_w13(e, f + 2)
                    low_w2(e, f)

            whole(program, pool)

        @block.tensor
        def _(pe):
            pe.sem_inc(up_summed, FREE * NH)
            pe.sem_inc(down_summed, FREE)

            def turn(e, m):
                for n in range(m * TB, (m + 1) * TB):
                    pe.wait_ge(norm_done, known(e * NT + (n + 1)))
                    pe.wait_ge(xT_low, known(e * NT + (n - 1)))
                    for c in range(C):
                        mm = pe.transpose(turn_ps[n % 2][:, c, :], xt[:, m % 2, n % TB, c * P:(c + 1) * P], ident[:])
                    mm.then_inc(turned, 1)

            def products(bank, w, f, cols):
                for c in range(C):
                    hi, lo = w13_hi[:, f % R, w, c, :], w13_lo[:, f % R, w, c, :]
                    pe.matmul(bank[:], hi, xT_hi[:, c, cols], start=(c == 0), stop=False)
                    pe.matmul(bank[:], hi, xT_lo[:, c, cols], start=False, stop=False)
                    mm = pe.matmul(bank[:], lo, xT_hi[:, c, cols], start=False, stop=(c == C - 1))
                return mm

            def gate_up(e):
                pe.wait_ge(xT_low, known(e * NT + NT))
                for f in range(FC):
                    pe.wait_ge(w13_low, known((e * FC + (f + 1)) * 2))
                    for h in range(NH):
                        k = NH * f + h
                        cols = slice(h * T, (h + 1) * T)
                        pe.wait_ge(silu_made, known(e * (NH * FC) + (k - 1 + FREE)))
                        products(gate_ps[k % 2], 0, f, cols).then_inc(gate_summed, 1)
                        pe.wait_ge(hid_made, known(e * (NH * FC) + (k - 1 + FREE)))
                        mm = products(up_ps[k % 2], 1, f, cols)
                        mm.then_inc(up_summed, 1)

            def down(e, n):
                pe.wait_ge(hid_low, known(e * NT + (n + 1 + FREE)))
                pe.wait_ge(out_made, known(e * NT + (n - 1 + FREE)))
                for f in range(FC):
                    if n == 0:
                        pe.wait_ge(w2_low, known(e * FC + (f + 1)))
                    hi, lo = hid_hi[:, n % 2, f, :], hid_lo[:, n % 2, f, :]
                    pe.matmul(down_ps[n % 2][:], hi, w2_hi[:, f, :], start=(f == 0), stop=False)
                    pe.matmul(down_ps[n % 2][:], hi, w2_lo[:, f, :], start=False, stop=False)
                    mm = pe.matmul(down_ps[n % 2][:], lo, w2_hi[:, f, :], start=False, stop=(f == FC - 1))
                mm.then_inc(down_summed, 1)

            pe.wait_ge(id_made, 1)
            for m in range(B):
                turn(0, m)

            def program(e, more):
                gate_up(e)
                for n in range(NT):
                    down(e, n)
                    if more and n in LN_AT:
                        turn(e + 1, LN_AT.index(n))

            whole(program, pe)

        @block.scalar
        def _(act):
            f_ = nc.scalar.activation
            act.sem_inc(silu_made, FREE)

            def high_w13(e, f):
                prev = ring(f, R)
                e, f = e + f // FC, f % FC
                act.wait_ge(w13_loaded[f % 2], known(nth_load(e, f) * 32))
                act.wait_ge(up_summed, known((e * FC + (prev + 1)) * NH + FREE * NH))
                for n in range(2):
                    f_(w13_hi[:, f % R, n], w13_in[:, f % 2, n], ACT.Copy).then_inc(w13_high, 1)

            def high_w2(e, f):
                act.wait_ge(w2_loaded[f % 2], known(nth_load(e, f) * 16))
                if f == 0:
                    act.wait_ge(down_summed, known(e * NT + FREE))
                f_(w2_hi[:, f], w2_in[:, f % 2], ACT.Copy).then_inc(w2_high, 1)

            def x_rstd(e, m):
                act.wait_ge(stat_done, known(e * B + (m + 1)))
                f_(lnv[:], mv[:, :, 1], ACT.Ln, bias=ln_eps[:]).then_inc(log_done, 1)
                act.wait_ge(log_done, known(e * B + (m + 1)))
                f_(rstd[:], lnv[:], ACT.Exp, scale=-0.5).then_inc(rstd_done, 1)

            def turned_high(e, m):
                for n in range(m * TB, (m + 1) * TB):
                    act.wait_ge(turned, known(e * NT + (n + 1)))
                    f_(xT_hi[:, :, n * P:(n + 1) * P], turn_ps[n % 2][:], ACT.Copy).then_inc(xT_high, 1)

            def silu(e, k):
                act.wait_ge(gate_summed, known(e * (NH * FC) + (k + 1)))
                act.wait_ge(hid_made, known(e * (NH * FC) + (k - 1 + FREE)))
                f_(gated[:, k % 2], gate_ps[k % 2][:], ACT.Silu).then_inc(silu_made, 1)

            def hidden_high(e, n):
                if n in (0, NT // NH):
                    act.wait_ge(hid_made, e * (NH * FC) + (NH * FC - NH + (n // (NT // NH) + 1) + FREE))
                act.wait_ge(down_summed, known(e * NT + (n - 1 + FREE)))
                f_(hid_hi[:, n % 2], hid[:, :, n * P:(n + 1) * P], ACT.Copy).then_inc(hid_high, 1)

            act.preload_act_table_set(LOG_EXP)
            act.wait_ge(eps_made, 1)
            for m in range(B):
                x_rstd(0, m)
                turned_high(0, m)
                if m < 2:
                    high_w13(0, m)

            def program(e, more):
                for f in range(FC):
                    for h in range(NH):
                        if (f, h) == (FC - 1, 1):
                            hidden_high(e, 0)
                            hidden_high(e, 1)
                        silu(e, NH * f + h)
                    if more or f + 2 < FC:
                        high_w13(e, f + 2)
                    high_w2(e, f)
                act.preload_act_table_set(LOG_EXP)
                for n in range(NT):
                    if n >= 2:
                        hidden_high(e, n)
                    if more and n - 2 in LN_AT:
                        turned_high(e + 1, LN_AT.index(n - 2))
                    if more and n in LN_AT:
                        x_rstd(e + 1, LN_AT.index(n))

            whole(program, act)

        @block.vector
        def _(dve):
            v = nc.vector
            v.memset(ln_eps[:], LN_EPS).then_inc(eps_made, 1)
            dve.sem_inc(hid_made, FREE)
            dve.sem_inc(hid_low, FREE)
            dve.sem_inc(out_made, FREE)

            def x_stats(e, m):
                dve.wait_ge(xt_loaded[m % 2], known((e * (B // 2) + (m // 2 + 1)) * 16))
                for t in range(TB):
                    v.bn_stats(bn[:, t], xt[:, m % 2, t]).then_inc(bn_done, 1)
                for t in range(TB):
                    dve.wait_ge(bn_done, e * NT + (m * TB + t + 1))
                    dve.sem_inc(passed, 1)
                    ins = v.bn_aggr(mv[:, t], bn[:, t])
                ins.then_inc(stat_done, 1)

            def x_norm(e, m):
                dve.wait_ge(rstd_done, known(e * B + (m + 1)))
                for t in range(TB):
                    v.tensor_scalar(xt[:, m % 2, t], xt[:, m % 2, t], mv[:, t, 0:1], rstd[:, t:t + 1],
                                    ALU.subtract, ALU.mult).then_inc(norm_done, 1)

            def turned_low(e, m):
                for n in range(m * TB, (m + 1) * TB):
                    cols = slice(n * P, (n + 1) * P)
                    dve.wait_ge(xT_high, known(e * NT + (n + 1)))
                    v.tensor_tensor(xT_lo[:, :, cols], turn_ps[n % 2][:], xT_hi[:, :, cols].bitcast(F32),
                                    ALU.subtract).then_inc(xT_low, 1)

            def hidden(e, k):
                f, h = divmod(k, NH)
                dve.wait_ge(silu_made, known(e * (NH * FC) + (k + 1 + FREE)))
                dve.wait_ge(up_summed, known(e * (NH * FC) + (k + 1 + NH * FREE)))
                if k == 0:
                    dve.wait_ge(hid_low, known(e * NT + FREE))
                v.tensor_tensor(hid[:, f, h * T:(h + 1) * T], up_ps[k % 2][:], gated[:, k % 2],
                                ALU.mult).then_inc(hid_made, 1)

            def hidden_low(e, n):
                dve.wait_ge(hid_high, known(e * NT + (n + 1)))
                v.tensor_tensor(hid_lo[:, n % 2], hid[:, :, n * P:(n + 1) * P], hid_hi[:, n % 2].bitcast(F32),
                                ALU.subtract).then_inc(hid_low, 1)

            def residual(e, n):
                dve.wait_ge(down_summed, known(e * NT + (n + 1 + FREE)))
                dve.wait_ge(res_loaded[n % 2], known((e * (NT // 2) + (n // 2 + 1)) * 16))
                dve.wait_ge(out_stored[n % 2], known((e * (NT // 2) + (n // 2 + FREE)) * 16))
                v.tensor_tensor(xout[:, n % 2], down_ps[n % 2][:], xres[:, n % 2], ALU.add).then_inc(out_made, 1)

            for m in range(B):
                x_stats(0, m)
                x_norm(0, m)
                turned_low(0, m)

            def program(e, more):
                for k in range(NH * FC):
                    if k == NH * FC - 1:
                        hidden_low(e, 0)
                        hidden_low(e, 1)
                    hidden(e, k)
                for n in range(NT):
                    if n >= 2:
                        hidden_low(e, n)
                    if n >= 2:
                        residual(e, n - 2)
                    if more and n - 2 in LN_AT:
                        turned_low(e + 1, LN_AT.index(n - 2))
                    if more and n in LN_AT:
                        x_stats(e + 1, LN_AT.index(n))
                        x_norm(e + 1, LN_AT.index(n))
                residual(e, NT - 2)
                residual(e, NT - 1)

            whole(program, dve)


def kernel(**inputs):
    import numpy as np
    import concourse.bacc as bacc
    from concourse.bass_utils import run_bass_kernel_spmd

    nc = bacc.Bacc("TRN2", target_bir_lowering=False, num_devices=1)
    arrays, args = {}, {}

    def give(name, array):
        array = np.ascontiguousarray(array)
        arrays[name] = array
        args[name] = nc.dram_tensor(name, array.shape, mybir.dt.from_np(array.dtype), kind="ExternalInput").ap()

    x = np.asarray(inputs["L0_attn_x"])
    B, S, D = x.shape
    give("x", x)
    for kind in "rkv":
        give("mix_" + kind, np.asarray(inputs["L0_attn_time_mix_" + kind]).reshape(D))
    for kind in "rkvo":
        give("wT_" + kind, np.asarray(inputs["L0_attn_W_" + kind]).T)
    for name in ("time_decay", "time_first", "ln_gamma", "ln_beta"):
        give(name, np.asarray(inputs["L0_attn_" + name]).reshape(D))
    for name in ("w1", "w3", "w2"):
        give(name, inputs["L0_ffn_" + name])
    out = nc.dram_tensor("out", (B * S, D), F32, kind="ExternalOutput").ap()
    x2 = nc.dram_tensor("x2", (B * S, D), F32, kind="Internal").ap()
    with ExitStack() as ctx:
        def sem(name):
            return ctx.enter_context(nc.semaphore(name))

        time_mixing(nc, sem, args["x"], [args["mix_" + k] for k in "kvr"], [args["wT_" + k] for k in "kvro"],
                    args["time_decay"], args["time_first"], args["ln_gamma"], args["ln_beta"], x2)
        feed_forward(nc, sem, x2, args["w1"], args["w3"], args["w2"], out, B, S)
    result = run_bass_kernel_spmd(nc, [arrays], core_ids=[0]).results[0]["out"]
    return result.reshape(B, S, D)
```

```python
from contextlib import ExitStack

import concourse.bass as bass
from concourse import mybir

ALU = mybir.AluOpType
ACT = mybir.ActivationFunctionType
F32 = mybir.dt.float32
F32R = mybir.dt.float32r

P = 128
T = 512
EPS = 1e-8
LN_EPS = 1e-5
LOWEST = -1e38
LOG_EXP = "natural_log_exp_and_others"
KIND_K, KIND_V, KIND_R = range(3)


def known(count):
    return max(count, 0) if isinstance(count, int) else count


FREE = 4


class Step:

    def __init__(self, b, i, per_batch):
        self.b, self.i, self.per_batch = b, i, per_batch

    def nth(self, n, of, ahead=0):
        return self.b * (self.per_batch * of) + ((self.i + ahead) * of + n)

    def nth_block(self):
        return self.b * self.per_batch + self.i if isinstance(self.b, int) else None


def time_mixing(nc, sem, x, mix_in, wT_in, decay_in, first_in, gamma_in, beta_in, x2):
    B, S, D = x.shape
    C = D // P
    HD = 32
    NB = S // T
    TT = T // P
    MIX = C - 1

    with ExitStack() as ctx:
        def sb(name, shape, dt=F32):
            return ctx.enter_context(nc.sbuf_tensor(name, shape, dt))

        def psum(name, shape):
            return ctx.enter_context(nc.psum_tensor(name, shape, F32))

        w_hi = sb("w_hi", [P, 4, C, D], F32R)
        w_lo = sb("w_lo", [P, 4, C, D], F32R)
        ident = sb("ident", [P, P])
        same_head = sb("same_head", [P, P])
        eps = sb("eps", [P, 1])
        ln_eps = sb("ln_eps", [P, 1])
        mixc = sb("mixc", [P, 3, C])
        decay = sb("decay", [P, C])
        neg_decay = sb("neg_decay", [P, C])
        bonus = sb("bonus", [P, C])
        neg_bonus = sb("neg_bonus", [P, C])
        gamma = sb("gamma", [P, C])
        beta = sb("beta", [P, C])
        xin = sb("xin", [P, 2, D])
        bn_x = sb("bn_x", [P, 2, 6])
        mv_x = sb("mv_x", [P, 2, 2])
        ln_x = sb("ln_x", [P, 2])
        rstd_x = sb("rstd_x", [P, 2])
        xT = sb("xT", [P, C, 1 + T])
        xd = sb("xd", [P, C, T])
        mixed = sb("mixed", [P, MIX, T])
        mix_hi = sb("mix_hi", [P, C, T], F32R)
        mix_lo = sb("mix_lo", [P, C, T], F32R)
        kk = sb("kk", [P, C, T])
        vv = sb("vv", [P, C, T])
        sig = sb("sig", [P, C, T])
        M = sb("M", [P, 2, 1 + T])
        A = sb("A", [P, 2, T])
        E = sb("E", [P, 2, T])
        S_ = sb("S_", [P, 2, 1 + T])
        acc = sb("acc", [P, 2, 1 + T])
        peak_c = sb("peak_c", [P, C])
        mass_c = sb("mass_c", [P, C])
        logm_c = sb("logm_c", [P, C])
        acc_c = sb("acc_c", [P, C])
        rw = sb("rw", [P, C, S])
        bn_rw = sb("bn_rw", [P, C, NB, 6])
        mv_rw = sb("mv_rw", [P, 2, C])
        mv_head = sb("mv_head", [P, 2, C])
        dev = sb("dev", [P, C])
        dev2 = sb("dev2", [P, C])
        var_h = sb("var_h", [P, C])
        ln_h = sb("ln_h", [P, C])
        rstd_h = sb("rstd_h", [P, C])
        scale_h = sb("scale_h", [P, C])
        mean_s = sb("mean_s", [P, C])
        shift_h = sb("shift_h", [P, C])
        y = sb("y", [P, C, T])
        y_hi = sb("y_hi", [P, 2, C, P], F32R)
        y_lo = sb("y_lo", [P, 2, C, P], F32R)
        xres = sb("xres", [P, 2, D])
        xout = sb("xout", [P, 1, D])

        acc_ps = [psum(f"acc_ps{g}", [P, T]) for g in range(C)]
        tp_ps = [psum(f"tp_ps{n}", [P, C, P]) for n in range(2)]
        out_ps = [psum(f"out_ps{n}", [P, D]) for n in range(2)]

        passed = sem("passed")
        const_loaded = sem("const_loaded")
        w_loaded = [sem(f"w_loaded{n}") for n in range(4)]
        acc_start = sem("acc_start")
        x_loaded, xres_loaded = ([sem(f"{name}{n}") for n in range(2)] for name in ("x_loaded", "xres_loaded"))
        x2_stored = sem("x2_stored")
        tail_stored = [sem(f"tail_stored{n}") for n in range(TT)]
        (ident_zero, ident_made, w_hi_made, w_lo_kr, w_lo_vo, decay_exp, const_made, bonus_neg) = map(
            sem, ("ident_zero", "ident_made", "w_hi_made", "w_lo_kr", "w_lo_vo", "decay_exp", "const_made", "bonus_neg"))
        (xbn, xstat, xlog, xrstd, xnormed, x_turned, shift_kept, xT_made, diff_made, diff2_made) = map(
            sem, ("xbn", "xstat", "xlog", "xrstd", "xnormed", "x_turned", "shift_kept", "xT_made", "diff_made",
                  "diff2_made"))
        (mix_made, hi_made, lo_made, chunk_used, kind_summed, kind_out) = map(
            sem, ("mix_made", "hi_made", "lo_made", "chunk_used", "kind_summed", "kind_out"))
        (start_set, peak_in, peak_made, peak_kept, fade_arg, fade_made, fresh_arg, fresh_made,
         mass_made, mass_kept, log_made, logm_in, logm_made, logm_kept, gap_made) = map(
            sem, ("start_set", "peak_in", "peak_made", "peak_kept", "fade_arg", "fade_made", "fresh_arg", "fresh_made",
                  "mass_made", "mass_kept", "log_made", "logm_in", "logm_made", "logm_kept", "gap_made"))
        (keep_made, add_made, e1_made, e2_made, keep_arg, addv_made, acc_in, acc_made, acc_kept,
         e1_arg, e2_arg, add_arg, den_made, e1a_made, e2v_made, num_made, gated, den_log, den_inv, rw_made, rw_bn) = map(
            sem, ("keep_made", "add_made", "e1_made", "e2_made", "keep_arg", "addv_made", "acc_in", "acc_made", "acc_kept",
                  "e1_arg", "e2_arg", "add_arg", "den_made", "e1a_made", "e2v_made", "num_made", "gated", "den_log", "den_inv",
                  "rw_made", "rw_bn"))
        (chan_stats, head_sum, head_copied, dev_made, dev_sq, dev_sum, head_var, head_log, head_rstd,
         scale_made, shift_mul, shift_made, y_made, yhi_made, ylo_made, out_summed, x2_made) = map(
            sem, ("chan_stats", "head_sum", "head_copied", "dev_made", "dev_sq", "dev_sum", "head_var", "head_log",
                  "head_rstd", "scale_made", "shift_mul", "shift_made", "y_made", "yhi_made", "ylo_made",
                  "out_summed", "x2_made"))

        x_tiles = x.rearrange("b (n p) d -> (b n) p d", p=P)
        x2_tiles = x2.rearrange("(n p) d -> n p d", p=P)

        def in_tail(s):
            return s.nth_block() is not None and s.nth_block() >= B * NB

        stage = [rw[:, :, n * D:(n + 1) * D] for n in range(4)]

        def whole(program, eng):
            program(0, True, True, False)
            with eng.Fori(1, B - 1) as b:
                program(b, True, True, True)
            program(B - 1, True, False, True)
            program(B, False, False, True)


        block = ctx.enter_context(nc.Block())

        @block.sync
        def _(sp):
            def load_x(s, n):
                sp.wait_ge(x_turned, known(s.nth(n - 1, TT)))
                tile = x_tiles[bass.ds(s.b * (NB * TT) + (s.i * TT + n), 1)]
                sp.dma_start(xin[:, n % 2:n % 2 + 1, :], tile.rearrange("o p d -> p o d")).then_inc(x_loaded[n % 2], 16)

            first = Step(0, 0, NB)
            load_x(first, 0)
            load_x(first, 1)
            with nc.allow_non_contiguous_dma(reason="per-channel vectors, once"):
                for n, m in enumerate(mix_in):
                    sp.dma_start(mixc[:, n, :], m.rearrange("(c p) -> p c", p=P)).then_inc(const_loaded, 16)
                for tile, src in ((decay, decay_in), (bonus, first_in), (gamma, gamma_in), (beta, beta_in)):
                    sp.dma_start(tile[:], src.rearrange("(c p) -> p c", p=P)).then_inc(const_loaded, 16)
            for n in range(4):
                sp.dma_start(stage[n], wT_in[n].rearrange("(c p) d -> p c d", p=P)).then_inc(w_loaded[n], 16)
                if n == 0:
                    load_x(first, 2)
                    load_x(first, 3)
            load_x(Step(0, 1, NB), 0)
            load_x(Step(0, 1, NB), 1)
            sp.sem_inc(x2_stored, 16 * FREE)

            def load_residual(s, n):
                sp.wait_ge(x2_made, known(s.nth(n - 1, TT, -NB) + FREE))
                tile = x_tiles[bass.ds(s.b * (NB * TT) + ((s.i - NB) * TT + n), 1)]
                sp.dma_start(xres[:, n % 2:n % 2 + 1, :], tile.rearrange("o p d -> p o d")).then_inc(xres_loaded[n % 2], 16)

            def store(s, n):
                sp.wait_ge(x2_made, known(s.nth(n + 1, TT, -NB) + FREE))
                tile = x2_tiles[bass.ds(s.b * (NB * TT) + ((s.i - NB) * TT + n), 1)]
                if in_tail(s):
                    sp.dma_start(tile.rearrange("o p d -> p o d"), kk[:, n:n + 1, :]).then_inc(tail_stored[n], 16)
                else:
                    sp.dma_start(tile.rearrange("o p d -> p o d"), xout[:]).then_inc(x2_stored, 16)

            def program(b, here, more, behind):
                for i in range(NB):
                    s, nxt, after = (Step(b, i + n, NB) for n in (0, 1, 2))
                    if behind:
                        load_residual(s, 0)
                        load_residual(s, 1)
                    if here and (more or i < NB - 1):
                        load_x(nxt, 2)
                        load_x(nxt, 3)
                    if here and (more or i < NB - 2):
                        load_x(after, 0)
                        load_x(after, 1)
                    if behind:
                        store(s, 0)
                        load_residual(s, 2)
                        store(s, 1)
                        load_residual(s, 3)
                        store(s, 2)
                        store(s, 3)

            whole(program, sp)
            sp.wait_ge(x2_stored, 16 * ((B - 1) * NB * TT + FREE))
            for stored in tail_stored:
                sp.wait_ge(stored, 16 * NB)

        @block.gpsimd
        def _(pool):
            g_ = nc.gpsimd
            g_.memset(ident[:], 0.0).then_inc(ident_zero, 1)
            g_.memset(same_head[:], 1.0 / HD).then_inc(ident_zero, 1)
            pool.wait_ge(ident_zero, 2)
            g_.affine_select(out=ident[:], in_=ident[:], compare_op=ALU.not_equal, fill=1.0, base=0,
                             pattern=[[-1, P]], channel_multiplier=1).then_inc(ident_made, 1)
            heads = same_head[:].rearrange("p (h k) -> p h k", k=HD)
            g_.affine_select(out=heads, in_=heads, compare_op=ALU.is_ge, fill=0.0, base=0,
                             pattern=[[-HD, P // HD], [0, HD]], channel_multiplier=1).then_inc(ident_made, 1)
            pool.wait_ge(ident_made, 2)
            g_.affine_select(out=heads, in_=heads, compare_op=ALU.is_ge, fill=0.0, base=HD - 1,
                             pattern=[[HD, P // HD], [0, HD]], channel_multiplier=-1).then_inc(ident_made, 1)

            def weight_low(n):
                for c in range(C):
                    pool.wait_ge(w_hi_made, C * n + c + 1)
                    g_.tensor_tensor(w_lo[:, n, c, :], stage[n][:, c, :], w_hi[:, n, c, :].bitcast(F32),
                                     ALU.subtract).then_inc(w_lo_kr, 1)

            def mix_low(s, kind, c):
                pool.wait_ge(hi_made, known(s.nth(C * kind + c + 1, 3 * C)))
                g_.tensor_tensor(mix_lo[:, c, :], mixed[:, c % MIX, :], mix_hi[:, c, :].bitcast(F32),
                                 ALU.subtract).then_inc(lo_made, 1)

            def difference(s):
                pool.wait_ge(xT_made, known(s.nth(TT, TT)))
                for c in range(C // 2, C):
                    g_.tensor_tensor(xd[:, c, :], xT[:, c, 1:], xT[:, c, 0:T], ALU.subtract).then_inc(diff2_made, 1)

            def fresh_argument(s, g):
                pool.wait_ge(peak_made, known(s.nth(g + 1, C)))
                pool.wait_ge(acc_made, known(s.nth(g - 1, C)))
                g_.tensor_tensor(E[:, g % 2, :], kk[:, g, :], M[:, g % 2, 1:], ALU.subtract).then_inc(fresh_arg, 1)

            def log_mass(s, g):
                pool.wait_ge(log_made, known(s.nth(g + 1, C)))
                g_.tensor_tensor(S_[:, g % 2, 1:], M[:, g % 2, 1:], S_[:, g % 2, 1:], ALU.add).then_inc(logm_made, 1)

            def weigh_acc(s, g):
                pool.wait_ge(den_made, known(s.nth(g + 1, C)))
                pool.wait_ge(acc_kept, known(s.nth(g + 1, C)))
                g_.tensor_tensor(S_[:, g % 2, 1:], S_[:, g % 2, 1:], acc[:, g % 2, 0:T], ALU.mult).then_inc(e1a_made, 1)

            def weigh_v(s, g):
                pool.wait_ge(den_made, known(s.nth(g + 1, C)))
                g_.tensor_tensor(M[:, g % 2, 0:T], M[:, g % 2, 0:T], vv[:, g, :], ALU.mult).then_inc(e2v_made, 1)

            def gate(s, g):
                rows = slice(s.i % NB * T, (s.i % NB + 1) * T)
                pool.wait_ge(kind_out, known(s.nth(C * KIND_R + g + 1, 3 * C)))
                pool.wait_ge(rw_made, known(s.nth(g + 1, C)))
                g_.tensor_tensor(rw[:, g, rows], rw[:, g, rows], sig[:, g, :], ALU.mult).then_inc(gated, 1)

            def y_low(s, n):
                pool.wait_ge(yhi_made, known(s.nth(n + 1, TT, -NB)))
                g_.tensor_tensor(y_lo[:, n % 2], y[:, :, n * P:(n + 1) * P], y_hi[:, n % 2].bitcast(F32),
                                 ALU.subtract).then_inc(ylo_made, 1)

            def program(b, here, more, behind):
                for i in range(NB):
                    last, s, nxt = (Step(b, i + n, NB) for n in (-1, 0, 1))
                    before = behind if i == 0 else here
                    ahead = here and (more or i < NB - 1)
                    if here:
                        mix_low(s, KIND_V, 0)
                        mix_low(s, KIND_V, 1)
                        mix_low(s, KIND_V, 2)
                        fresh_argument(s, 0)
                        mix_low(s, KIND_V, 3)
                    if before:
                        weigh_acc(last, 3)
                        weigh_v(last, 3)
                    if here:
                        log_mass(s, 0)
                    if before:
                        gate(last, 2)
                    if here:
                        mix_low(s, KIND_R, 0)
                    if before:
                        gate(last, 3)
                    if here:
                        fresh_argument(s, 1)
                        mix_low(s, KIND_R, 1)
                        mix_low(s, KIND_R, 2)
                        mix_low(s, KIND_R, 3)
                        log_mass(s, 1)
                        weigh_acc(s, 0)
                        weigh_v(s, 0)
                    if behind:
                        y_low(s, 0)
                        y_low(s, 1)
                    if here:
                        fresh_argument(s, 2)
                    if ahead:
                        difference(nxt)
                    if behind:
                        y_low(s, 2)
                    if here:
                        weigh_acc(s, 1)
                        weigh_v(s, 1)
                    if behind:
                        y_low(s, 3)
                    if here:
                        log_mass(s, 2)
                    if ahead:
                        mix_low(nxt, KIND_K, 0)
                    if here:
                        fresh_argument(s, 3)
                        gate(s, 0)
                        gate(s, 1)
                    if ahead:
                        mix_low(nxt, KIND_K, 1)
                    if here:
                        log_mass(s, 3)
                    if ahead:
                        mix_low(nxt, KIND_K, 2)
                        mix_low(nxt, KIND_K, 3)
                    if here:
                        weigh_acc(s, 2)
                        weigh_v(s, 2)

            first = Step(0, 0, NB)
            pool.sem_inc(ylo_made, FREE)
            weight_low(KIND_K)
            difference(first)
            mix_low(first, KIND_K, 0)
            mix_low(first, KIND_K, 1)
            mix_low(first, KIND_K, 2)
            mix_low(first, KIND_K, 3)
            weight_low(KIND_R)
            whole(program, pool)

        @block.tensor
        def _(pe):
            def turn(s, n):
                pe.wait_ge(xnormed, known(s.nth(n + 1, TT)))
                pe.wait_ge(xT_made, known(s.nth(n - 1, TT)))
                for c in range(C):
                    mm = pe.transpose(tp_ps[n % 2][:, c, :], xin[:, n % 2, c * P:(c + 1) * P], ident[:])
                mm.then_inc(x_turned, 1)

            def project(s, kind, c):
                if s.nth_block() == 0 and c == 0:
                    pe.wait_ge(w_lo_kr, 2 * C if kind == KIND_R else C)
                    if kind != KIND_K:
                        pe.wait_ge(w_lo_vo, 2 * C if kind == KIND_R else C)
                pe.wait_ge(lo_made, known(s.nth(C * kind + c + 1, 3 * C)))
                for g in range(C):
                    if c == 0:
                        pe.wait_ge(kind_out, known(s.nth(C * kind + g + 1 - C, 3 * C)))
                    cols = slice(g * P, (g + 1) * P)
                    hi, lo = w_hi[:, kind, c, cols], w_lo[:, kind, c, cols]
                    pe.matmul(acc_ps[g][:], hi, mix_hi[:, c, :], start=(c == 0), stop=False)
                    pe.matmul(acc_ps[g][:], hi, mix_lo[:, c, :], start=False, stop=False)
                    mm = pe.matmul(acc_ps[g][:], lo, mix_hi[:, c, :], start=False, stop=(c == C - 1))
                    if c == C - 1:
                        mm.then_inc(kind_summed, 1)
                if c < C - 1:
                    mm.then_inc(chunk_used, 1)

            def head_means(b):
                pe.wait_ge(chan_stats, b * 1)
                pe.wait_ge(x2_made, known(Step(b, 0, NB).nth(-1, TT, -NB) + FREE))
                pe.matmul(out_ps[0][:, 0:2 * C], same_head[:], mv_rw[:].rearrange("p a c -> p (a c)"),
                          start=True, stop=True).then_inc(head_sum, 1)

            def head_squares(b):
                pe.wait_ge(dev_sq, b * 1)
                pe.matmul(out_ps[0][:, 2 * C:3 * C], same_head[:], dev2[:], start=True, stop=True).then_inc(dev_sum, 1)

            def out_product(s, n):
                if n == 0:
                    pe.wait_ge(head_var, s.b * 1)
                pe.wait_ge(ylo_made, known(s.nth(n + 1, TT, -NB) + FREE))
                pe.wait_ge(x2_made, known(s.nth(n - 1, TT, -NB) + FREE))
                for g in range(C):
                    hi, lo = y_hi[:, n % 2, g, :], y_lo[:, n % 2, g, :]
                    pe.matmul(out_ps[n % 2][:], hi, w_hi[:, 3, g, :], start=(g == 0), stop=False)
                    pe.matmul(out_ps[n % 2][:], hi, w_lo[:, 3, g, :], start=False, stop=False)
                    mm = pe.matmul(out_ps[n % 2][:], lo, w_hi[:, 3, g, :], start=False, stop=(g == C - 1))
                mm.then_inc(out_summed, 1)

            def program(b, here, more, behind):
                for i in range(NB):
                    last, s, nxt = (Step(b, i + n, NB) for n in (-1, 0, 1))
                    before = behind if i == 0 else here
                    ahead = here and (more or i < NB - 1)
                    if here:
                        project(s, KIND_K, 1)
                        project(s, KIND_K, 2)
                        project(s, KIND_K, 3)
                        project(s, KIND_V, 0)
                        project(s, KIND_V, 1)
                        project(s, KIND_V, 2)
                        project(s, KIND_V, 3)
                        project(s, KIND_R, 0)
                    if behind and i == 0:
                        head_means(b)
                    if ahead:
                        turn(nxt, 0)
                        turn(nxt, 1)
                    if behind and i == 0:
                        head_squares(b)
                    if here:
                        project(s, KIND_R, 1)
                        project(s, KIND_R, 2)
                    if ahead:
                        turn(nxt, 2)
                        turn(nxt, 3)
                    if behind:
                        out_product(s, 0)
                        out_product(s, 1)
                    if here:
                        project(s, KIND_R, 3)
                    if behind:
                        out_product(s, 2)
                        out_product(s, 3)
                    if ahead:
                        project(nxt, KIND_K, 0)

            first = Step(0, 0, NB)
            pe.sem_inc(out_summed, FREE)
            pe.wait_ge(ident_made, 3)
            turn(first, 0)
            turn(first, 1)
            turn(first, 2)
            turn(first, 3)
            project(first, KIND_K, 0)
            whole(program, pe)

        @block.scalar
        def _(act):
            f = nc.scalar.activation
            act.preload_act_table_set(LOG_EXP)

            def copy_turned(s, n):
                act.wait_ge(x_turned, known(s.nth(n + 1, TT)))
                if n == 0:
                    act.wait_ge(shift_kept, known(s.nth(1, 1)))
                f(xT[:, :, 1 + n * P:1 + (n + 1) * P], tp_ps[n % 2][:], ACT.Copy).then_inc(xT_made, 1)

            def x_rstd(s, pair):
                act.wait_ge(xstat, known(s.nth(pair + 1, 2)))
                f(ln_x[:], mv_x[:, :, 1], ACT.Ln, bias=ln_eps[:]).then_inc(xlog, 1)
                act.wait_ge(xlog, known(s.nth(pair + 1, 2)))
                f(rstd_x[:], ln_x[:], ACT.Exp, scale=-0.5).then_inc(xrstd, 1)

            def mix_high(s, kind, c):
                act.wait_ge(mix_made, known(s.nth(C * kind + c + 1, 3 * C)))
                if c < C - 1:
                    act.wait_ge(chunk_used, known(s.nth((C - 1) * (kind - 1) + c + 1, 3 * (C - 1))))
                else:
                    act.wait_ge(kind_summed, known(s.nth(C * kind, 3 * C)))
                f(mix_hi[:, c, :], mixed[:, c % MIX, :], ACT.Copy).then_inc(hi_made, 1)

            def copy_k(s, g):
                act.wait_ge(kind_summed, known(s.nth(C * KIND_K + g + 1, 3 * C)))
                act.wait_ge(gap_made, known(s.nth(g + 1, C, -1)))
                f(kk[:, g, :], acc_ps[g][:], ACT.Copy).then_inc(kind_out, 1)

            def copy_v(s, g):
                act.wait_ge(kind_summed, known(s.nth(C * KIND_V + g + 1, 3 * C)))
                act.wait_ge(e2v_made, known(s.nth(g + 1, C, -1)))
                f(vv[:, g, :], acc_ps[g][:], ACT.Copy).then_inc(kind_out, 1)

            def copy_r(s):
                for g in range(C):
                    act.wait_ge(kind_summed, known(s.nth(C * KIND_R + g + 1, 3 * C)))
                    act.wait_ge(gated, known(s.nth(g + 1, C, -1)))
                    f(sig[:, g, :], acc_ps[g][:], ACT.Sigmoid).then_inc(kind_out, 1)
                act.preload_act_table_set(LOG_EXP)

            def fade(s, g):
                act.wait_ge(fade_arg, known(s.nth(g + 1, C)))
                f(A[:, g % 2, :], A[:, g % 2, :], ACT.Exp).then_inc(fade_made, 1)

            def fresh(s, g):
                act.wait_ge(fresh_arg, known(s.nth(g + 1, C)))
                f(E[:, g % 2, :], E[:, g % 2, :], ACT.Exp).then_inc(fresh_made, 1)

            def mass_log(s, g):
                act.wait_ge(mass_kept, known(s.nth(g + 1, C)))
                f(S_[:, g % 2, 1:], S_[:, g % 2, 1:], ACT.Ln, bias=eps[:]).then_inc(log_made, 1)

            def e1_argument(s, g):
                act.wait_ge(logm_kept, known(s.nth(g + 1, C)))
                f(S_[:, g % 2, 1:], M[:, g % 2, 0:T], ACT.Relu, bias=bonus[:, g:g + 1], scale=-1.0).then_inc(e1_arg, 1)

            def keep(s, g):
                act.wait_ge(keep_arg, known(s.nth(g + 1, C)))
                f(A[:, g % 2, :], A[:, g % 2, :], ACT.Exp).then_inc(keep_made, 1)

            def add(s, g):
                act.wait_ge(add_arg, known(s.nth(g + 1, C)))
                f(E[:, g % 2, :], E[:, g % 2, :], ACT.Exp, scale=-1.0).then_inc(add_made, 1)

            def e2_argument(s, g):
                act.wait_ge(e1_arg, known(s.nth(g + 1, C)))
                act.wait_ge(keep_arg, known(s.nth(g + 1, C)))
                act.wait_ge(add_arg, known(s.nth(g + 1, C)))
                f(M[:, g % 2, 0:T], M[:, g % 2, 0:T], ACT.Relu, bias=neg_bonus[:, g:g + 1]).then_inc(e2_arg, 1)

            def e1(s, g):
                act.wait_ge(e1_arg, known(s.nth(g + 1, C)))
                f(S_[:, g % 2, 1:], S_[:, g % 2, 1:], ACT.Exp, scale=-1.0).then_inc(e1_made, 1)

            def e2(s, g):
                act.wait_ge(e2_arg, known(s.nth(g + 1, C)))
                f(M[:, g % 2, 0:T], M[:, g % 2, 0:T], ACT.Exp, scale=-1.0).then_inc(e2_made, 1)

            def log_denominator(s, g):
                act.wait_ge(den_made, known(s.nth(g + 1, C)))
                f(A[:, g % 2, :], A[:, g % 2, :], ACT.Ln).then_inc(den_log, 1)

            def inverse(s, g):
                act.wait_ge(den_log, known(s.nth(g + 1, C)))
                f(A[:, g % 2, :], A[:, g % 2, :], ACT.Exp, scale=-1.0).then_inc(den_inv, 1)

            def head_rstds(b):
                act.wait_ge(head_var, b * 1)
                f(ln_h[:], var_h[:], ACT.Ln, bias=ln_eps[:]).then_inc(head_log, 1)
                act.wait_ge(head_log, b * 1)
                f(rstd_h[:], ln_h[:], ACT.Exp, scale=-0.5).then_inc(head_rstd, 1)

            def normed(s):
                if s.i == 0:
                    act.wait_ge(shift_made, s.b * 1)
                act.wait_ge(ylo_made, known(s.nth(TT, TT, -NB - 1) + FREE))
                for g in range(C):
                    f(y[:, g, :], rw[:, g, s.i * T:(s.i + 1) * T], ACT.Identity,
                      bias=shift_h[:, g:g + 1], scale=scale_h[:, g:g + 1]).then_inc(y_made, 1)

            def y_high(s, n):
                act.wait_ge(y_made, known(s.nth(C, C, -NB) + FREE))
                act.wait_ge(out_summed, known(s.nth(n - 1, TT, -NB) + FREE))
                f(y_hi[:, n % 2], y[:, :, n * P:(n + 1) * P], ACT.Copy).then_inc(yhi_made, 1)

            def program(b, here, more, behind):
                for i in range(NB):
                    last, s, nxt = (Step(b, i + n, NB) for n in (-1, 0, 1))
                    before = behind if i == 0 else here
                    ahead = here and (more or i < NB - 1)
                    if here:
                        mix_high(s, KIND_V, 0)
                    if before:
                        e1(last, 3)
                    if here:
                        mix_high(s, KIND_V, 1)
                        copy_k(s, 0)
                        mix_high(s, KIND_V, 2)
                    if before:
                        inverse(last, 2)
                    if here:
                        copy_k(s, 1)
                        copy_k(s, 2)
                    if before:
                        e2_argument(last, 3)
                    if here:
                        copy_k(s, 3)
                    if before:
                        e2(last, 3)
                    if here:
                        mix_high(s, KIND_V, 3)
                        fade(s, 0)
                        fresh(s, 0)
                    if ahead:
                        x_rstd(nxt, 0)
                    if here:
                        mass_log(s, 0)
                        mix_high(s, KIND_R, 0)
                        mix_high(s, KIND_R, 1)
                    if before:
                        log_denominator(last, 3)
                        inverse(last, 3)
                    if here:
                        mix_high(s, KIND_R, 2)
                        e1_argument(s, 0)
                        copy_v(s, 0)
                        e1(s, 0)
                        copy_v(s, 1)
                        copy_v(s, 2)
                        keep(s, 0)
                        fade(s, 1)
                        copy_v(s, 3)
                        add(s, 0)
                        fresh(s, 1)
                        e2_argument(s, 0)
                        mix_high(s, KIND_R, 3)
                    if ahead:
                        copy_turned(nxt, 0)
                    if behind and i == 0:
                        head_rstds(b)
                    if here:
                        mass_log(s, 1)
                        e2(s, 0)
                    if behind:
                        normed(s)
                        y_high(s, 0)
                    if ahead:
                        x_rstd(nxt, 1)
                        copy_turned(nxt, 1)
                    if here:
                        log_denominator(s, 0)
                    if behind:
                        y_high(s, 1)
                    if here:
                        inverse(s, 0)
                        keep(s, 1)
                    if ahead:
                        copy_turned(nxt, 2)
                    if here:
                        add(s, 1)
                    if ahead:
                        copy_turned(nxt, 3)
                    if here:
                        e1_argument(s, 1)
                        e2_argument(s, 1)
                        e1(s, 1)
                    if behind:
                        y_high(s, 2)
                    if here:
                        e2(s, 1)
                        fade(s, 2)
                        fresh(s, 2)
                        log_denominator(s, 1)
                    if behind:
                        y_high(s, 3)
                    if here:
                        inverse(s, 1)
                    if ahead:
                        mix_high(nxt, KIND_K, 0)
                    if here:
                        mass_log(s, 2)
                        copy_r(s)
                        fade(s, 3)
                        fresh(s, 3)
                        keep(s, 2)
                    if ahead:
                        mix_high(nxt, KIND_K, 1)
                    if here:
                        e1_argument(s, 2)
                        add(s, 2)
                        mass_log(s, 3)
                    if ahead:
                        mix_high(nxt, KIND_K, 2)
                    if here:
                        e2_argument(s, 2)
                        e1(s, 2)
                    if ahead:
                        mix_high(nxt, KIND_K, 3)
                    if here:
                        e2(s, 2)
                        e1_argument(s, 3)
                        keep(s, 3)
                        log_denominator(s, 2)
                        add(s, 3)

            def weight_high(n):
                act.wait_ge(w_loaded[n], 16)
                for c in range(C):
                    f(w_hi[:, n, c, :], stage[n][:, c, :], ACT.Copy).then_inc(w_hi_made, 1)

            first = Step(0, 0, NB)
            act.sem_inc(y_made, FREE)
            act.wait_ge(const_made, 2)
            x_rstd(first, 0)
            act.wait_ge(const_loaded, 16 * 7)
            f(neg_decay[:], decay[:], ACT.Exp).then_inc(decay_exp, 1)
            copy_turned(first, 0)
            copy_turned(first, 1)
            weight_high(KIND_K)
            x_rstd(first, 1)
            copy_turned(first, 2)
            copy_turned(first, 3)
            weight_high(KIND_V)
            mix_high(first, KIND_K, 0)
            mix_high(first, KIND_K, 1)
            mix_high(first, KIND_K, 2)
            mix_high(first, KIND_K, 3)
            weight_high(KIND_R)
            weight_high(3)
            whole(program, act)

        @block.vector
        def _(dve):
            v = nc.vector
            v.memset(eps[:], EPS).then_inc(const_made, 1)
            v.memset(ln_eps[:], LN_EPS).then_inc(const_made, 1)
            dve.sem_inc(x2_made, FREE)

            def x_stats(s, pair):
                for n in (2 * pair, 2 * pair + 1):
                    dve.wait_ge(x_loaded[n % 2], known(s.nth(n // 2 + 1, TT // 2) * 16))
                    v.bn_stats(bn_x[:, n % 2, :], xin[:, n % 2, :]).then_inc(xbn, 1)
                for n in (2 * pair, 2 * pair + 1):
                    dve.wait_ge(xbn, known(s.nth(n + 1, TT)))
                    dve.sem_inc(passed, 1)
                    ins = v.bn_aggr(mv_x[:, n % 2, :], bn_x[:, n % 2, :])
                ins.then_inc(xstat, 1)

            def x_norm(s, pair):
                dve.wait_ge(xrstd, known(s.nth(pair + 1, 2)))
                for n in (2 * pair, 2 * pair + 1):
                    v.tensor_scalar(xin[:, n % 2, :], xin[:, n % 2, :], mv_x[:, n % 2, 0:1], rstd_x[:, n % 2:n % 2 + 1],
                                    ALU.subtract, ALU.mult).then_inc(xnormed, 1)

            def keep_shift(s):
                dve.wait_ge(mix_made, known(s.nth(0, 3 * C)))
                if s.i % NB == 0:
                    v.memset(xT[:, :, 0:1], 0.0).then_inc(shift_kept, 1)
                else:
                    v.tensor_copy(xT[:, :, 0:1], xT[:, :, T:T + 1]).then_inc(shift_kept, 1)

            def difference(s):
                dve.wait_ge(xT_made, known(s.nth(TT, TT)))
                for c in range(C // 2):
                    v.tensor_tensor(xd[:, c, :], xT[:, c, 1:], xT[:, c, 0:T], ALU.subtract).then_inc(diff_made, 1)

            def mix(s, kind, c):
                if c < C // 2:
                    dve.wait_ge(diff_made, known(s.nth(c + 1, C // 2)))
                else:
                    dve.wait_ge(diff2_made, known(s.nth(c - C // 2 + 1, C // 2)))
                if c % MIX == 0:
                    dve.wait_ge(lo_made, known(s.nth(C * kind + c // MIX, 3 * C)))
                v.scalar_tensor_tensor(mixed[:, c % MIX, :], xd[:, c, :], mixc[:, kind, c:c + 1], xT[:, c, 0:T],
                                       ALU.mult, ALU.add).then_inc(mix_made, 1)

            def start_front():
                for tile, value in ((peak_c, LOWEST), (logm_c, LOWEST), (mass_c, 1.0)):
                    ins = v.memset(tile[:], value)
                ins.then_inc(start_set, 1)

            def peak(s, g):
                j = g % 2
                if s.i == 0 and g == 0:
                    dve.wait_ge(logm_kept, known(s.nth(0, C)))
                    start_front()
                    dve.wait_ge(start_set, s.b + 1)
                dve.wait_ge(num_made, known(s.nth(g - 1, C)))
                v.tensor_copy(M[:, j, 0:1], peak_c[:, g:g + 1]).then_inc(peak_in, 1)
                dve.wait_ge(kind_out, known(s.nth(C * KIND_K + g + 1, 3 * C)))
                v.tensor_tensor_scan(M[:, j, 1:], decay[:, g:g + 1].to_broadcast([P, T]), kk[:, g, :],
                                     peak_c[:, g:g + 1], ALU.add, ALU.max).then_inc(peak_made, 1)

            def fade(s, g):
                j = g % 2
                dve.wait_ge(peak_made, known(s.nth(g + 1, C)))
                dve.wait_ge(rw_made, known(s.nth(g - 1, C)))
                v.scalar_tensor_tensor(A[:, j, :], M[:, j, 0:T], decay[:, g:g + 1], M[:, j, 1:],
                                       ALU.add, ALU.subtract).then_inc(fade_arg, 1)
                v.tensor_copy(peak_c[:, g:g + 1], M[:, j, T:T + 1]).then_inc(peak_kept, 1)

            def mass(s, g):
                j = g % 2
                dve.wait_ge(fade_made, known(s.nth(g + 1, C)))
                dve.wait_ge(fresh_made, known(s.nth(g + 1, C)))
                v.tensor_tensor_scan(S_[:, j, 1:], A[:, j, :], E[:, j, :], mass_c[:, g:g + 1],
                                     ALU.mult, ALU.add).then_inc(mass_made, 1)
                v.tensor_copy(S_[:, j, 0:1], logm_c[:, g:g + 1]).then_inc(logm_in, 1)
                dve.wait_ge(mass_made, known(s.nth(g + 1, C)))
                v.tensor_copy(mass_c[:, g:g + 1], S_[:, j, T:T + 1]).then_inc(mass_kept, 1)

            def gap(s, g):
                j = g % 2
                dve.wait_ge(logm_made, known(s.nth(g + 1, C)))
                dve.wait_ge(peak_kept, known(s.nth(g + 1, C)))
                v.tensor_tensor(M[:, j, 0:T], S_[:, j, 0:T], kk[:, g, :], ALU.subtract).then_inc(gap_made, 1)
                v.tensor_copy(logm_c[:, g:g + 1], S_[:, j, T:T + 1]).then_inc(logm_kept, 1)

            def keep_argument(s, g):
                dve.wait_ge(gap_made, known(s.nth(g + 1, C)))
                v.tensor_scalar(A[:, g % 2, :], M[:, g % 2, 0:T], decay[:, g:g + 1], 0.0,
                                ALU.add, ALU.min).then_inc(keep_arg, 1)

            def add_argument(s, g):
                dve.wait_ge(gap_made, known(s.nth(g + 1, C)))
                v.tensor_scalar(E[:, g % 2, :], M[:, g % 2, 0:T], decay[:, g:g + 1], 0.0,
                                ALU.add, ALU.max).then_inc(add_arg, 1)

            def add_v(s, g):
                j = g % 2
                dve.wait_ge(kind_out, known(s.nth(C * KIND_V + g + 1, 3 * C)))
                dve.wait_ge(add_made, known(s.nth(g + 1, C)))
                v.tensor_tensor(E[:, j, :], E[:, j, :], vv[:, g, :], ALU.mult).then_inc(addv_made, 1)

            def accumulate(s, g):
                j = g % 2
                if s.i == 0 and g == 0:
                    dve.wait_ge(acc_kept, known(s.nth(0, C)))
                    v.memset(acc_c[:], 0.0).then_inc(acc_start, 1)
                    dve.wait_ge(acc_start, s.b + 1)
                dve.wait_ge(e1a_made, known(s.nth(g - 1, C)))
                v.tensor_copy(acc[:, j, 0:1], acc_c[:, g:g + 1]).then_inc(acc_in, 1)
                dve.wait_ge(keep_made, known(s.nth(g + 1, C)))
                dve.wait_ge(addv_made, known(s.nth(g + 1, C)))
                v.tensor_tensor_scan(acc[:, j, 1:], A[:, j, :], E[:, j, :], acc_c[:, g:g + 1],
                                     ALU.mult, ALU.add).then_inc(acc_made, 1)

            def denominator(s, g):
                j = g % 2
                dve.wait_ge(e1_made, known(s.nth(g + 1, C)))
                dve.wait_ge(e2_made, known(s.nth(g + 1, C)))
                dve.wait_ge(acc_made, known(s.nth(g + 1, C)))
                v.scalar_tensor_tensor(A[:, j, :], M[:, j, 0:T], EPS, S_[:, j, 1:],
                                       ALU.add, ALU.add).then_inc(den_made, 1)
                v.tensor_copy(acc_c[:, g:g + 1], acc[:, j, T:T + 1]).then_inc(acc_kept, 1)

            def numerator(s, g):
                j = g % 2
                dve.wait_ge(e1a_made, known(s.nth(g + 1, C)))
                dve.wait_ge(e2v_made, known(s.nth(g + 1, C)))
                v.tensor_tensor(S_[:, j, 1:], S_[:, j, 1:], M[:, j, 0:T], ALU.add).then_inc(num_made, 1)

            def result(s, g):
                j, rows = g % 2, slice(s.i % NB * T, (s.i % NB + 1) * T)
                dve.wait_ge(den_inv, known(s.nth(g + 1, C)))
                dve.wait_ge(num_made, known(s.nth(g + 1, C)))
                dve.wait_ge(y_made, known(s.nth(g + 1, C, -NB) + FREE))
                if s.nth_block() == 0 and g == 0:
                    dve.wait_ge(w_lo_kr, 2 * C)
                v.tensor_tensor(rw[:, g, rows], S_[:, j, 1:], A[:, j, :], ALU.mult).then_inc(rw_made, 1)

            def measure(s, g):
                rows = slice(s.i % NB * T, (s.i % NB + 1) * T)
                dve.wait_ge(gated, known(s.nth(g + 1, C)))
                v.bn_stats(bn_rw[:, g, s.i % NB, :], rw[:, g, rows]).then_inc(rw_bn, 1)

            def channel_stats(b):
                dve.wait_ge(rw_bn, b * (NB * C))
                dve.sem_inc(passed, 1)
                for g in range(C):
                    ins = v.bn_aggr(mv_rw[:, :, g], bn_rw[:, g].rearrange("p n k -> p (n k)"))
                ins.then_inc(chan_stats, 1)

            def head_deviation(b):
                dve.wait_ge(head_sum, b * 1)
                v.tensor_copy(mv_head[:].rearrange("p a c -> p (a c)"), out_ps[0][:, 0:2 * C]).then_inc(head_copied, 1)
                dve.wait_ge(head_copied, b * 1)
                v.tensor_tensor(dev[:], mv_rw[:, 0, :], mv_head[:, 0, :], ALU.subtract).then_inc(dev_made, 1)
                dve.wait_ge(dev_made, b * 1)
                v.tensor_tensor(dev2[:], dev[:], dev[:], ALU.mult).then_inc(dev_sq, 1)

            def head_variance(b):
                dve.wait_ge(dev_sum, b * 1)
                v.tensor_tensor(var_h[:], out_ps[0][:, 2 * C:3 * C], mv_head[:, 1, :], ALU.add).then_inc(head_var, 1)

            def head_affine(b):
                dve.wait_ge(head_rstd, b * 1)
                v.tensor_tensor(scale_h[:], rstd_h[:], gamma[:], ALU.mult).then_inc(scale_made, 1)
                dve.wait_ge(scale_made, b * 1)
                v.tensor_tensor(mean_s[:], mv_head[:, 0, :], scale_h[:], ALU.mult).then_inc(shift_mul, 1)
                dve.wait_ge(shift_mul, b * 1)
                v.tensor_tensor(shift_h[:], beta[:], mean_s[:], ALU.subtract).then_inc(shift_made, 1)

            def residual(s, n):
                dve.wait_ge(xres_loaded[n % 2], known(s.nth(n // 2 + 1, TT // 2, -NB) * 16))
                dve.wait_ge(out_summed, known(s.nth(n + 1, TT, -NB) + FREE))
                if in_tail(s):
                    if s.i == 0:
                        dve.wait_ge(gap_made, B * NB * C)
                    else:
                        dve.wait_ge(tail_stored[n], s.i * 16)
                    total = kk[:, n, :]
                else:
                    dve.wait_ge(x2_stored, known((s.nth(n, TT, -NB) + FREE) * 16))
                    total = xout[:, 0, :]
                v.tensor_tensor(total, out_ps[n % 2][:], xres[:, n % 2, :], ALU.add).then_inc(x2_made, 1)

            def program(b, here, more, behind):
                for i in range(NB):
                    last, s, nxt = (Step(b, i + n, NB) for n in (-1, 0, 1))
                    before = behind if i == 0 else here
                    ahead = here and (more or i < NB - 1)
                    if before:
                        accumulate(last, 3)
                        numerator(last, 2)
                    if here:
                        peak(s, 0)
                    if before:
                        result(last, 2)
                    if here:
                        mix(s, KIND_V, 3)
                        fade(s, 0)
                    if before:
                        denominator(last, 3)
                    if ahead:
                        x_stats(nxt, 0)
                    if here:
                        mass(s, 0)
                        mix(s, KIND_R, 0)
                        mix(s, KIND_R, 1)
                        mix(s, KIND_R, 2)
                    if before:
                        numerator(last, 3)
                    if here:
                        gap(s, 0)
                        peak(s, 1)
                    if before:
                        result(last, 3)
                        measure(last, 2)
                    if here:
                        keep_argument(s, 0)
                        fade(s, 1)
                    if before:
                        measure(last, 3)
                    if here:
                        add_argument(s, 0)
                    if behind and i == 0:
                        channel_stats(b)
                    if ahead:
                        x_norm(nxt, 0)
                    if here:
                        mix(s, KIND_R, 3)
                    if behind and i == 0:
                        head_deviation(b)
                    if ahead:
                        keep_shift(nxt)
                    if here:
                        mass(s, 1)
                    if behind and i == 0:
                        head_variance(b)
                    if here:
                        add_v(s, 0)
                    if behind and i == 0:
                        head_affine(b)
                    if here:
                        accumulate(s, 0)
                        denominator(s, 0)
                        gap(s, 1)
                    if ahead:
                        x_stats(nxt, 1)
                    if here:
                        add_argument(s, 1)
                        keep_argument(s, 1)
                    if ahead:
                        x_norm(nxt, 1)
                    if here:
                        numerator(s, 0)
                        peak(s, 2)
                        result(s, 0)
                        fade(s, 2)
                        add_v(s, 1)
                        accumulate(s, 1)
                    if behind:
                        residual(s, 0)
                    if ahead:
                        difference(nxt)
                    if here:
                        denominator(s, 1)
                    if ahead:
                        mix(nxt, KIND_K, 0)
                    if here:
                        mass(s, 2)
                    if ahead:
                        mix(nxt, KIND_K, 1)
                    if behind:
                        residual(s, 1)
                    if here:
                        numerator(s, 1)
                    if ahead:
                        mix(nxt, KIND_K, 2)
                    if here:
                        peak(s, 3)
                        result(s, 1)
                        gap(s, 2)
                        fade(s, 3)
                    if behind:
                        residual(s, 2)
                    if here:
                        keep_argument(s, 2)
                        add_argument(s, 2)
                    if ahead:
                        mix(nxt, KIND_K, 3)
                    if here:
                        mass(s, 3)
                        measure(s, 0)
                        measure(s, 1)
                        add_v(s, 2)
                    if behind:
                        residual(s, 3)
                    if here:
                        accumulate(s, 2)
                        gap(s, 3)
                        keep_argument(s, 3)
                        denominator(s, 2)
                        add_argument(s, 3)
                    if ahead:
                        mix(nxt, KIND_V, 0)
                        mix(nxt, KIND_V, 1)
                    if here:
                        add_v(s, 3)
                    if ahead:
                        mix(nxt, KIND_V, 2)

            def weight_low(n):
                for c in range(C):
                    dve.wait_ge(w_hi_made, C * n + c + 1)
                    v.tensor_tensor(w_lo[:, n, c, :], stage[n][:, c, :], w_hi[:, n, c, :].bitcast(F32),
                                    ALU.subtract).then_inc(w_lo_vo, 1)

            first = Step(0, 0, NB)
            x_stats(first, 0)
            x_norm(first, 0)
            dve.wait_ge(decay_exp, 1)
            v.tensor_scalar(decay[:], neg_decay[:], -1.0, None, ALU.mult)
            v.tensor_scalar(neg_bonus[:], bonus[:], -1.0, None, ALU.mult).then_inc(bonus_neg, 1)
            dve.wait_ge(bonus_neg, 1)
            keep_shift(first)
            x_stats(first, 1)
            x_norm(first, 1)
            difference(first)
            mix(first, KIND_K, 0)
            mix(first, KIND_K, 1)
            mix(first, KIND_K, 2)
            mix(first, KIND_K, 3)
            weight_low(KIND_V)
            mix(first, KIND_V, 0)
            mix(first, KIND_V, 1)
            mix(first, KIND_V, 2)
            weight_low(3)
            whole(program, dve)


def feed_forward(nc, sem, x2, w1, w3, w2, out, B, S):
    E, D, F = w1.shape
    C = D // P
    FC = F // P
    CAP = S // E
    N = B * CAP
    NT = N // P
    TB = CAP // P
    NH = N // T
    R = 3
    LN_AT = (0, 1, 3, 4)

    with ExitStack() as ctx:
        def sb(name, shape, dt=F32):
            return ctx.enter_context(nc.sbuf_tensor(name, shape, dt))

        def psum(name, shape):
            return ctx.enter_context(nc.psum_tensor(name, shape, F32))

        ident = sb("ident2", [P, P])
        ln_eps = sb("ln_eps2", [P, 1])
        w13_in = sb("w13_in", [P, 2, 2, C, P])
        w13_hi = sb("w13_hi", [P, R, 2, C, P], F32R)
        w13_lo = sb("w13_lo", [P, R, 2, C, P], F32R)
        w2_in = sb("w2_in", [P, 2, D])
        w2_hi = sb("w2_hi", [P, FC, D], F32R)
        w2_lo = sb("w2_lo", [P, FC, D], F32R)
        xt = sb("xt", [P, 2, TB, D])
        bn = sb("bn", [P, 2, TB, 6])
        mv = sb("mv", [P, 2, TB, 2])
        lnv = sb("lnv", [P, 2, TB])
        rstd = sb("rstd", [P, 2, TB])
        xT_hi = sb("xT_hi", [P, C, N], F32R)
        xT_lo = sb("xT_lo", [P, C, N], F32R)
        gated = sb("gated2", [P, 2, T])
        hid = sb("hid", [P, FC, N])
        hid_hi = sb("hid_hi", [P, 2, FC, P], F32R)
        hid_lo = sb("hid_lo", [P, 2, FC, P], F32R)
        xres = sb("xres2", [P, 2, D])
        xout = sb("xout2", [P, 2, D])

        gate_ps = [psum(f"gate_ps{n}", [P, T]) for n in range(2)]
        up_ps = [psum(f"up_ps{n}", [P, T]) for n in range(2)]
        turn_ps = [psum(f"turn_ps{n}", [P, C, P]) for n in range(2)]
        down_ps = [psum(f"down_ps{n}", [P, D]) for n in range(2)]

        passed = sem("passed2")
        w13_loaded, w2_loaded, xt_loaded, res_loaded, out_stored = (
            [sem(f"{name}{n}") for n in range(2)]
            for name in ("w13_loaded", "w2_loaded", "xt_loaded", "res_loaded", "out_stored"))
        (id_zero, id_made, eps_made, w13_high, w13_low, w2_high, w2_low) = map(
            sem, ("id_zero", "id_made", "eps_made", "w13_high", "w13_low", "w2_high", "w2_low"))
        (bn_done, stat_done, log_done, rstd_done, norm_done, turned, xT_high, xT_low) = map(
            sem, ("bn_done", "stat_done", "log_done", "rstd_done", "norm_done", "turned", "xT_high", "xT_low"))
        (gate_summed, up_summed, silu_made, hid_made, hid_high, hid_low, down_summed, out_made) = map(
            sem, ("gate_summed", "up_summed", "silu_made", "hid_made", "hid_high", "hid_low", "down_summed", "out_made"))

        def whole(program, eng):
            program(0, True, True)
            with eng.Fori(1, E - 1) as e:
                program(e, True, False)
            program(E - 1, False, False)

        def ring(f, slots):
            f %= FC
            if f >= slots:
                return f - slots
            return max(n for n in range(FC) if n % slots == f % slots) - FC

        def nth_load(e, f):
            return e * len(range(f % 2, FC, 2)) + (f // 2 + 1)

        def tokens(t, e, n, count=1):
            m, h = divmod(n, TB)
            tiles = t.rearrange("(n p) d -> n p d", p=P)
            return tiles[bass.ds(e * TB + (m * (S // P) + h), count)].rearrange("n p d -> p n d")

        block = ctx.enter_context(nc.Block())

        @block.sync
        def _(sp):
            for stored in out_stored:
                sp.sem_inc(stored, 16 * FREE)

            def load_w13(e, f):
                prev = ring(f, 2)
                e, f = e + f // FC, f % FC
                sp.wait_ge(w13_low, known((e * FC + (prev + 1)) * 2))
                for n, w in enumerate((w1, w3)):
                    src = w.rearrange("e (c p) f -> e p c f", p=P)[bass.ds(e, 1), :, :, f * P:(f + 1) * P]
                    sp.dma_start(w13_in[:, f % 2, n], src.rearrange("o p c f -> (o p) c f")).then_inc(w13_loaded[f % 2], 16)

            def load_w2(e, f):
                prev = ring(f, 2)
                e, f = e + f // FC, f % FC
                sp.wait_ge(w2_low, known(e * FC + (prev + 1)))
                src = w2[bass.ds(e, 1), f * P:(f + 1) * P, :]
                sp.dma_start(w2_in[:, f % 2], src.rearrange("o p d -> (o p) d")).then_inc(w2_loaded[f % 2], 16)

            def load_xt(e, m):
                sp.wait_ge(turned, known(e * NT + (m - 1) * TB))
                sp.dma_start(xt[:, m % 2], tokens(x2, e, m * TB, TB)).then_inc(xt_loaded[m % 2], 16)

            load_xt(0, 0)
            load_xt(0, 1)
            load_w13(0, 0)
            load_xt(0, 2)
            load_w13(0, 1)
            load_xt(0, 3)
            load_w2(0, 0)
            load_w2(0, 1)
            load_w13(0, 2)

            def program(e, more, first):
                for f in range(FC):
                    if more and f in (4, 5):
                        load_xt(e + 1, f - 4)
                    if more or f + 3 < FC:
                        load_w13(e, f + 3)
                    if more or f + 2 < FC:
                        load_w2(e, f + 2)
                for n in range(NT + 2):
                    if n < NT:
                        sp.wait_ge(out_made, known(e * NT + (n - 1 + FREE)))
                        sp.dma_start(xres[:, n % 2:n % 2 + 1], tokens(x2, e, n)).then_inc(res_loaded[n % 2], 16)
                    if 2 <= n < B and more:
                        load_xt(e + 1, n)
                    if n >= 2:
                        sp.wait_ge(out_made, known(e * NT + (n - 1 + FREE)))
                        sp.dma_start(tokens(out, e, n - 2), xout[:, n % 2:n % 2 + 1]).then_inc(out_stored[n % 2], 16)

            whole(program, sp)
            for stored in out_stored:
                sp.wait_ge(stored, 16 * (E * NT // 2 + FREE))

        @block.gpsimd
        def _(pool):
            g_ = nc.gpsimd
            g_.memset(ident[:], 0.0).then_inc(id_zero, 1)
            pool.wait_ge(id_zero, 1)
            g_.affine_select(out=ident[:], in_=ident[:], compare_op=ALU.not_equal, fill=1.0, base=0,
                             pattern=[[-1, P]], channel_multiplier=1).then_inc(id_made, 1)

            def low_w13(e, f):
                e, f = e + f // FC, f % FC
                pool.wait_ge(w13_high, known((e * FC + f + 1) * 2))
                for n in range(2):
                    g_.tensor_tensor(w13_lo[:, f % R, n], w13_in[:, f % 2, n], w13_hi[:, f % R, n].bitcast(F32),
                                     ALU.subtract).then_inc(w13_low, 1)

            def low_w2(e, f):
                pool.wait_ge(w2_high, known(e * FC + (f + 1)))
                g_.tensor_tensor(w2_lo[:, f], w2_in[:, f % 2], w2_hi[:, f].bitcast(F32), ALU.subtract).then_inc(w2_low, 1)

            low_w13(0, 0)
            low_w13(0, 1)

            def program(e, more, first):
                for f in range(FC):
                    if more or f + 2 < FC:
                        low_w13(e, f + 2)
                    low_w2(e, f)

            whole(program, pool)

        @block.tensor
        def _(pe):
            pe.sem_inc(up_summed, FREE * NH)
            pe.sem_inc(down_summed, FREE)

            def turn(e, m):
                for n in range(m * TB, (m + 1) * TB):
                    pe.wait_ge(norm_done, known(e * NT + (n + 1)))
                    pe.wait_ge(xT_low, known(e * NT + (n - 1)))
                    for c in range(C):
                        mm = pe.transpose(turn_ps[n % 2][:, c, :], xt[:, m % 2, n % TB, c * P:(c + 1) * P], ident[:])
                    mm.then_inc(turned, 1)

            def products(bank, w, f, cols):
                for c in range(C):
                    hi, lo = w13_hi[:, f % R, w, c, :], w13_lo[:, f % R, w, c, :]
                    pe.matmul(bank[:], hi, xT_hi[:, c, cols], start=(c == 0), stop=False)
                    pe.matmul(bank[:], hi, xT_lo[:, c, cols], start=False, stop=False)
                    mm = pe.matmul(bank[:], lo, xT_hi[:, c, cols], start=False, stop=(c == C - 1))
                return mm

            def gate_up(e, first):
                pe.wait_ge(xT_low, known(e * NT + (NT // NH if first else NT)))
                for f in range(FC):
                    pe.wait_ge(w13_low, known((e * FC + (f + 1)) * 2))
                    for h in range(NH):
                        k = NH * f + h
                        cols = slice(h * T, (h + 1) * T)
                        pe.wait_ge(silu_made, known(e * (NH * FC) + (k - 1 + FREE)))
                        products(gate_ps[k % 2], 0, f, cols).then_inc(gate_summed, 1)
                        pe.wait_ge(hid_made, known(e * (NH * FC) + (k - 1 + FREE)))
                        products(up_ps[k % 2], 1, f, cols).then_inc(up_summed, 1)
                        if first and k == 0:
                            for m in range(B // NH, B):
                                turn(e, m)
                            pe.wait_ge(xT_low, NT)

            def down(e, n):
                pe.wait_ge(hid_low, known(e * NT + (n + 1 + FREE)))
                pe.wait_ge(out_made, known(e * NT + (n - 1 + FREE)))
                for f in range(FC):
                    if n == 0:
                        pe.wait_ge(w2_low, known(e * FC + (f + 1)))
                    hi, lo = hid_hi[:, n % 2, f, :], hid_lo[:, n % 2, f, :]
                    pe.matmul(down_ps[n % 2][:], hi, w2_hi[:, f, :], start=(f == 0), stop=False)
                    pe.matmul(down_ps[n % 2][:], hi, w2_lo[:, f, :], start=False, stop=False)
                    mm = pe.matmul(down_ps[n % 2][:], lo, w2_hi[:, f, :], start=False, stop=(f == FC - 1))
                mm.then_inc(down_summed, 1)

            pe.wait_ge(id_made, 1)
            for m in range(B // NH):
                turn(0, m)

            def program(e, more, first):
                gate_up(e, first)
                for n in range(NT):
                    down(e, n)
                    if more and n in LN_AT:
                        turn(e + 1, LN_AT.index(n))

            whole(program, pe)

        @block.scalar
        def _(act):
            f_ = nc.scalar.activation
            act.sem_inc(silu_made, FREE)

            def high_w13(e, f):
                prev = ring(f, R)
                e, f = e + f // FC, f % FC
                act.wait_ge(w13_loaded[f % 2], known(nth_load(e, f) * 32))
                act.wait_ge(up_summed, known((e * FC + (prev + 1)) * NH + FREE * NH))
                for n in range(2):
                    f_(w13_hi[:, f % R, n], w13_in[:, f % 2, n], ACT.Copy).then_inc(w13_high, 1)

            def high_w2(e, f):
                act.wait_ge(w2_loaded[f % 2], known(nth_load(e, f) * 16))
                if f == 0:
                    act.wait_ge(down_summed, known(e * NT + FREE))
                f_(w2_hi[:, f], w2_in[:, f % 2], ACT.Copy).then_inc(w2_high, 1)

            def x_rstd(e, m):
                act.wait_ge(stat_done, known(e * B + (m + 1)))
                f_(lnv[:, m % 2], mv[:, m % 2, :, 1], ACT.Ln, bias=ln_eps[:]).then_inc(log_done, 1)
                act.wait_ge(log_done, known(e * B + (m + 1)))
                f_(rstd[:, m % 2], lnv[:, m % 2], ACT.Exp, scale=-0.5).then_inc(rstd_done, 1)

            def turned_high(e, m):
                for n in range(m * TB, (m + 1) * TB):
                    act.wait_ge(turned, known(e * NT + (n + 1)))
                    f_(xT_hi[:, :, n * P:(n + 1) * P], turn_ps[n % 2][:], ACT.Copy).then_inc(xT_high, 1)

            def silu(e, k):
                act.wait_ge(gate_summed, known(e * (NH * FC) + (k + 1)))
                act.wait_ge(hid_made, known(e * (NH * FC) + (k - 1 + FREE)))
                f_(gated[:, k % 2], gate_ps[k % 2][:], ACT.Silu).then_inc(silu_made, 1)

            def hidden_high(e, n):
                if n in (0, NT // NH):
                    act.wait_ge(hid_made, e * (NH * FC) + (NH * FC - NH + (n // (NT // NH) + 1) + FREE))
                act.wait_ge(down_summed, known(e * NT + (n - 1 + FREE)))
                f_(hid_hi[:, n % 2], hid[:, :, n * P:(n + 1) * P], ACT.Copy).then_inc(hid_high, 1)

            act.preload_act_table_set(LOG_EXP)
            act.wait_ge(eps_made, 1)
            for batches in (range(B // NH), range(B // NH, B)):
                for m in batches:
                    x_rstd(0, m)
                if batches[0] == 0:
                    for m in batches:
                        turned_high(0, m)
                        high_w13(0, m)

            def program(e, more, first):
                for f in range(FC):
                    for h in range(NH):
                        if (f, h) == (FC - 1, 1):
                            hidden_high(e, 0)
                            hidden_high(e, 1)
                        silu(e, NH * f + h)
                        if first and (f, h) == (0, 0):
                            for m in range(B // NH, B):
                                turned_high(e, m)
                    if more or f + 2 < FC:
                        high_w13(e, f + 2)
                    high_w2(e, f)
                act.preload_act_table_set(LOG_EXP)
                for n in range(NT):
                    if n >= 2:
                        hidden_high(e, n)
                    if more and n - 2 in LN_AT:
                        turned_high(e + 1, LN_AT.index(n - 2))
                    if more and n in LN_AT:
                        x_rstd(e + 1, LN_AT.index(n))

            whole(program, act)

        @block.vector
        def _(dve):
            v = nc.vector
            v.memset(ln_eps[:], LN_EPS).then_inc(eps_made, 1)
            dve.sem_inc(hid_made, FREE)
            dve.sem_inc(hid_low, FREE)
            dve.sem_inc(out_made, FREE)

            def x_stats(e, m):
                dve.wait_ge(xt_loaded[m % 2], known((e * (B // 2) + (m // 2 + 1)) * 16))
                for t in range(TB):
                    v.bn_stats(bn[:, m % 2, t], xt[:, m % 2, t]).then_inc(bn_done, 1)
                for t in range(TB):
                    dve.wait_ge(bn_done, e * NT + (m * TB + t + 1))
                    dve.sem_inc(passed, 1)
                    ins = v.bn_aggr(mv[:, m % 2, t], bn[:, m % 2, t])
                ins.then_inc(stat_done, 1)

            def x_norm(e, m):
                dve.wait_ge(rstd_done, known(e * B + (m + 1)))
                for t in range(TB):
                    v.tensor_scalar(xt[:, m % 2, t], xt[:, m % 2, t], mv[:, m % 2, t, 0:1], rstd[:, m % 2, t:t + 1],
                                    ALU.subtract, ALU.mult).then_inc(norm_done, 1)

            def turned_low(e, m):
                for n in range(m * TB, (m + 1) * TB):
                    cols = slice(n * P, (n + 1) * P)
                    dve.wait_ge(xT_high, known(e * NT + (n + 1)))
                    v.tensor_tensor(xT_lo[:, :, cols], turn_ps[n % 2][:], xT_hi[:, :, cols].bitcast(F32),
                                    ALU.subtract).then_inc(xT_low, 1)

            def hidden(e, k):
                f, h = divmod(k, NH)
                dve.wait_ge(silu_made, known(e * (NH * FC) + (k + 1 + FREE)))
                dve.wait_ge(up_summed, known(e * (NH * FC) + (k + 1 + NH * FREE)))
                if k == 0:
                    dve.wait_ge(hid_low, known(e * NT + FREE))
                v.tensor_tensor(hid[:, f, h * T:(h + 1) * T], up_ps[k % 2][:], gated[:, k % 2],
                                ALU.mult).then_inc(hid_made, 1)

            def hidden_low(e, n):
                dve.wait_ge(hid_high, known(e * NT + (n + 1)))
                v.tensor_tensor(hid_lo[:, n % 2], hid[:, :, n * P:(n + 1) * P], hid_hi[:, n % 2].bitcast(F32),
                                ALU.subtract).then_inc(hid_low, 1)

            def residual(e, n):
                dve.wait_ge(down_summed, known(e * NT + (n + 1 + FREE)))
                dve.wait_ge(res_loaded[n % 2], known((e * (NT // 2) + (n // 2 + 1)) * 16))
                dve.wait_ge(out_stored[n % 2], known((e * (NT // 2) + (n // 2 + FREE)) * 16))
                v.tensor_tensor(xout[:, n % 2], down_ps[n % 2][:], xres[:, n % 2], ALU.add).then_inc(out_made, 1)

            for batches in (range(B // NH), range(B // NH, B)):
                for m in batches:
                    x_stats(0, m)
                    x_norm(0, m)
                if batches[0] == 0:
                    for m in batches:
                        turned_low(0, m)

            def program(e, more, first):
                for k in range(NH * FC):
                    if k == NH * FC - 1:
                        hidden_low(e, 0)
                        hidden_low(e, 1)
                    hidden(e, k)
                    if first and k == 0:
                        for m in range(B // NH, B):
                            turned_low(e, m)
                for n in range(NT):
                    if n >= 2:
                        hidden_low(e, n)
                    if n >= 2:
                        residual(e, n - 2)
                    if more and n - 2 in LN_AT:
                        turned_low(e + 1, LN_AT.index(n - 2))
                    if more and n in LN_AT:
                        x_stats(e + 1, LN_AT.index(n))
                        x_norm(e + 1, LN_AT.index(n))
                residual(e, NT - 2)
                residual(e, NT - 1)

            whole(program, dve)


def kernel(**inputs):
    import numpy as np
    import concourse.bacc as bacc
    from concourse.bass_utils import run_bass_kernel_spmd

    nc = bacc.Bacc("TRN2", target_bir_lowering=False, num_devices=1)
    arrays, args = {}, {}

    def give(name, array):
        array = np.ascontiguousarray(array)
        arrays[name] = array
        args[name] = nc.dram_tensor(name, array.shape, mybir.dt.from_np(array.dtype), kind="ExternalInput").ap()

    x = np.asarray(inputs["L0_attn_x"])
    B, S, D = x.shape
    give("x", x)
    for kind in "rkv":
        give("mix_" + kind, np.asarray(inputs["L0_attn_time_mix_" + kind]).reshape(D))
    for kind in "rkvo":
        give("wT_" + kind, np.asarray(inputs["L0_attn_W_" + kind]).T)
    for name in ("time_decay", "time_first", "ln_gamma", "ln_beta"):
        give(name, np.asarray(inputs["L0_attn_" + name]).reshape(D))
    for name in ("w1", "w3", "w2"):
        give(name, inputs["L0_ffn_" + name])
    out = nc.dram_tensor("out", (B * S, D), F32, kind="ExternalOutput").ap()
    x2 = nc.dram_tensor("x2", (B * S, D), F32, kind="Internal").ap()
    with ExitStack() as ctx:
        def sem(name):
            return ctx.enter_context(nc.semaphore(name))

        time_mixing(nc, sem, args["x"], [args["mix_" + k] for k in "kvr"], [args["wT_" + k] for k in "kvro"],
                    args["time_decay"], args["time_first"], args["ln_gamma"], args["ln_beta"], x2)
        feed_forward(nc, sem, x2, args["w1"], args["w3"], args["w2"], out, B, S)
    result = run_bass_kernel_spmd(nc, [arrays], core_ids=[0]).results[0]["out"]
    return result.reshape(B, S, D)
```
